# Optimizing a Trainium2 kernel written in Bass

```python
import numpy as np
import jax
import jax.numpy as jnp

def _softmax(x, axis=-1):
    return jax.nn.softmax(x, axis=axis)

def _gelu(x):
    return jax.nn.gelu(x, approximate=True)

def _silu(x):
    return jax.nn.silu(x)

def _sigmoid(x):
    return jax.nn.sigmoid(x)

def _layernorm(x, axis=-1, eps=1e-05):
    m = jnp.mean(x, axis=axis, keepdims=True)
    v = jnp.var(x, axis=axis, keepdims=True)
    return (x - m) / jnp.sqrt(v + eps)

def _scatter_add(tgt, idx, src, axis=0):
    return tgt.at[idx].add(src)

def _segment_sum(src, seg, n):
    return jax.ops.segment_sum(src, seg, n)
kernel_name = 'mk_cond_seq_d2_seqx_r2_e56039'

def setup_inputs(seed: int=0):
    np.random.seed(seed)
    _w = jnp.asarray

    def _rec_inputs():
        import jax
        import jax.numpy as jnp
        _rk = jax.random.key(seed)
        x = 7.22e-05 + 1 * jax.random.normal(jax.random.fold_in(_rk, 1), (8, 1024, 512), jnp.float32)
        _lenS = 1024 - jax.random.randint(jax.random.fold_in(_rk, 7), (8,), 0, max(1, 1024 // 4) + 1, jnp.int32)
        _lenS2 = 1024 - jax.random.randint(jax.random.fold_in(_rk, 8), (8,), 0, max(1, 1024 // 4) + 1, jnp.int32)
        cond_1024 = 0.0061147 + 1.02565 * jax.random.normal(jax.random.fold_in(_rk, 11), (8, 512), jnp.float32)
        return (x, cond_1024)
    x, cond_1024 = _rec_inputs()

    def _L0_cond_setup():
        import jax, jax.numpy as jnp
        import numpy as np
        D = 512
        H = 16
        HD = D // H
        MLP = 4 * D

        def _lin(key, fin, fout):
            k1, k2 = jax.random.split(key)
            lim = 1.0 / np.sqrt(fin)
            W = jax.random.uniform(k1, (fin, fout), minval=-lim, maxval=lim, dtype=jnp.float32)
            b = jax.random.uniform(k2, (fout,), minval=-lim, maxval=lim, dtype=jnp.float32)
            return (W, b)

        def layernorm(x, g, b, eps=1e-05):
            mu = jnp.mean(x, axis=-1, keepdims=True)
            var = jnp.var(x, axis=-1, keepdims=True)
            return (x - mu) * jax.lax.rsqrt(var + eps) * g + b

        def attention(h, Wqkv, bqkv, Wproj, bproj):
            B, L, _ = h.shape
            qkv = (h @ Wqkv + bqkv).reshape(B, L, 3, H, HD)
            q, k, v = jnp.moveaxis(qkv, 2, 0)
            scale = HD ** (-0.5)
            attn = jnp.einsum('blhd,bmhd->bhlm', q, k) * scale
            attn = jax.nn.softmax(attn, axis=-1)
            out = jnp.einsum('bhlm,bmhd->blhd', attn, v).reshape(B, L, D)
            return out @ Wproj + bproj
        key = jax.random.key(seed)
        ks = jax.random.split(key, 10)
        x = jax.random.normal(ks[0], (4, 1024, D), dtype=jnp.float32)
        time_emb = jax.random.normal(ks[1], (4, D), dtype=jnp.float32)
        Wqkv, bqkv = _lin(ks[2], D, 3 * D)
        Wproj, bproj = _lin(ks[3], D, D)
        W1, b1 = _lin(ks[4], D, MLP)
        W2, b2 = _lin(ks[5], MLP, D)
        Wt, bt = _lin(ks[6], D, 6 * D)
        g1 = jnp.ones((D,), jnp.float32)
        be1 = jnp.zeros((D,), jnp.float32)
        g2 = jnp.ones((D,), jnp.float32)
        be2 = jnp.zeros((D,), jnp.float32)
        return {'x': x, 'time_emb': time_emb, 'Wqkv': Wqkv, 'bqkv': bqkv, 'Wproj': Wproj, 'bproj': bproj, 'W1': W1, 'b1': b1, 'W2': W2, 'b2': b2, 'Wt': Wt, 'bt': bt, 'g1': g1, 'be1': be1, 'g2': g2, 'be2': be2}
    _L0_cond_all = _L0_cond_setup()
    _L0_cond_in = {k: v for k, v in _L0_cond_all.items() if k in ('Wqkv', 'bqkv', 'Wproj', 'bproj', 'W1', 'b1', 'W2', 'b2', 'Wt', 'bt', 'g1', 'be1', 'g2', 'be2')}
    del _L0_cond_all

    def _L1_cond_setup():
        import jax, jax.numpy as jnp
        import numpy as np
        EPS_RMS = 1e-06
        EPS_Q = 1e-05

        def _weight_quant(w):
            scale = 1.0 / jnp.clip(jnp.mean(jnp.abs(w)), EPS_Q)
            wq = jnp.clip(jnp.round(w * scale), -1.0, 1.0) / scale
            return w + jax.lax.stop_gradient(wq - w)

        def _activation_quant(x):
            scale = 127.0 / jnp.clip(jnp.max(jnp.abs(x), axis=-1, keepdims=True), EPS_Q)
            xq = jnp.clip(jnp.round(x * scale), -128.0, 127.0) / scale
            return x + jax.lax.stop_gradient(xq - x)

        def _rmsnorm(x, weight):
            inv = jax.lax.rsqrt(jnp.mean(x * x, axis=-1, keepdims=True) + EPS_RMS)
            return x * inv * weight
        key = jax.random.key(seed)
        k1, k2, k3 = jax.random.split(key, 3)
        B, S, D, CD = (8, 2048, 512, 512)
        x = jax.random.normal(k1, (B, S, D), dtype=jnp.float32)
        c = jax.random.normal(k2, (B, CD), dtype=jnp.float32)
        w_proj = jax.random.normal(k3, (2 * D, CD), dtype=jnp.float32) * 0.02
        b_proj = jnp.zeros((2 * D,), dtype=jnp.float32)
        rms_weight = jnp.ones((D,), dtype=jnp.float32)
        return {'x': x, 'c': c, 'w_proj': w_proj, 'b_proj': b_proj, 'rms_weight': rms_weight}
    _L1_cond_all = _L1_cond_setup()
    _L1_cond_in = {k: v for k, v in _L1_cond_all.items() if k in ('w_proj', 'b_proj', 'rms_weight')}
    del _L1_cond_all
    return {'x': x, 'cond_1024': cond_1024, 'L0_cond_Wqkv': _L0_cond_in['Wqkv'], 'L0_cond_bqkv': _L0_cond_in['bqkv'], 'L0_cond_Wproj': _L0_cond_in['Wproj'], 'L0_cond_bproj': _L0_cond_in['bproj'], 'L0_cond_W1': _L0_cond_in['W1'], 'L0_cond_b1': _L0_cond_in['b1'], 'L0_cond_W2': _L0_cond_in['W2'], 'L0_cond_b2': _L0_cond_in['b2'], 'L0_cond_Wt': _L0_cond_in['Wt'], 'L0_cond_bt': _L0_cond_in['bt'], 'L0_cond_g1': _L0_cond_in['g1'], 'L0_cond_be1': _L0_cond_in['be1'], 'L0_cond_g2': _L0_cond_in['g2'], 'L0_cond_be2': _L0_cond_in['be2'], 'L1_cond_w_proj': _L1_cond_in['w_proj'], 'L1_cond_b_proj': _L1_cond_in['b_proj'], 'L1_cond_rms_weight': _L1_cond_in['rms_weight']}

def reference(x, cond_1024, L0_cond_Wqkv, L0_cond_bqkv, L0_cond_Wproj, L0_cond_bproj, L0_cond_W1, L0_cond_b1, L0_cond_W2, L0_cond_b2, L0_cond_Wt, L0_cond_bt, L0_cond_g1, L0_cond_be1, L0_cond_g2, L0_cond_be2, L1_cond_w_proj, L1_cond_b_proj, L1_cond_rms_weight):
    import jax
    import jax.numpy as jnp

    def _L0_cond_ref(x, time_emb, Wqkv, bqkv, Wproj, bproj, W1, b1, W2, b2, Wt, bt, g1, be1, g2, be2):
        import jax, jax.numpy as jnp
        import numpy as np
        D = 512
        H = 16
        HD = D // H
        MLP = 4 * D

        def _lin(key, fin, fout):
            k1, k2 = jax.random.split(key)
            lim = 1.0 / np.sqrt(fin)
            W = jax.random.uniform(k1, (fin, fout), minval=-lim, maxval=lim, dtype=jnp.float32)
            b = jax.random.uniform(k2, (fout,), minval=-lim, maxval=lim, dtype=jnp.float32)
            return (W, b)

        def layernorm(x, g, b, eps=1e-05):
            mu = jnp.mean(x, axis=-1, keepdims=True)
            var = jnp.var(x, axis=-1, keepdims=True)
            return (x - mu) * jax.lax.rsqrt(var + eps) * g + b

        def attention(h, Wqkv, bqkv, Wproj, bproj):
            B, L, _ = h.shape
            qkv = (h @ Wqkv + bqkv).reshape(B, L, 3, H, HD)
            q, k, v = jnp.moveaxis(qkv, 2, 0)
            scale = HD ** (-0.5)
            attn = jnp.einsum('blhd,bmhd->bhlm', q, k) * scale
            attn = jax.nn.softmax(attn, axis=-1)
            out = jnp.einsum('bhlm,bmhd->blhd', attn, v).reshape(B, L, D)
            return out @ Wproj + bproj
        tp = (jax.nn.silu(time_emb) @ Wt + bt)[:, None, :]
        shift_msa, scale_msa, gate_msa, shift_mlp, scale_mlp, gate_mlp = jnp.split(tp, 6, axis=-1)
        h = layernorm(x, g1, be1)
        h = h * (1.0 + scale_msa) + shift_msa
        h = attention(h, Wqkv, bqkv, Wproj, bproj)
        x = x + gate_msa * h
        h = layernorm(x, g2, be2)
        h = h * (1.0 + scale_mlp) + shift_mlp
        h = jax.nn.gelu(h @ W1 + b1, approximate=False) @ W2 + b2
        x = x + gate_mlp * h
        return x

    def _L1_cond_ref(x, c, w_proj, b_proj, rms_weight):
        import jax, jax.numpy as jnp
        import numpy as np
        EPS_RMS = 1e-06
        EPS_Q = 1e-05

        def _weight_quant(w):
            scale = 1.0 / jnp.clip(jnp.mean(jnp.abs(w)), EPS_Q)
            wq = jnp.clip(jnp.round(w * scale), -1.0, 1.0) / scale
            return w + jax.lax.stop_gradient(wq - w)

        def _activation_quant(x):
            scale = 127.0 / jnp.clip(jnp.max(jnp.abs(x), axis=-1, keepdims=True), EPS_Q)
            xq = jnp.clip(jnp.round(x * scale), -128.0, 127.0) / scale
            return x + jax.lax.stop_gradient(xq - x)

        def _rmsnorm(x, weight):
            inv = jax.lax.rsqrt(jnp.mean(x * x, axis=-1, keepdims=True) + EPS_RMS)
            return x * inv * weight
        if c.ndim == 2:
            c = c[:, None, :]
        cq = _activation_quant(c)
        wq = _weight_quant(w_proj)
        emb = jnp.einsum('btc,dc->btd', cq, wq) + b_proj
        scale, shift = jnp.split(emb, 2, axis=-1)
        xn = _rmsnorm(x, rms_weight)
        return xn * (1.0 + scale) + shift
    x = _L0_cond_ref(x, cond_1024, L0_cond_Wqkv, L0_cond_bqkv, L0_cond_Wproj, L0_cond_bproj, L0_cond_W1, L0_cond_b1, L0_cond_W2, L0_cond_b2, L0_cond_Wt, L0_cond_bt, L0_cond_g1, L0_cond_be1, L0_cond_g2, L0_cond_be2)
    x = _L1_cond_ref(x, cond_1024, L1_cond_w_proj, L1_cond_b_proj, L1_cond_rms_weight)
    return x

_drawn_inputs = setup_inputs


def setup_inputs(seed=0):
    import zlib

    import numpy as np

    out = dict(_drawn_inputs(seed))
    spreads = {'L0_cond_g1': (1.0, 0.6),
     'L0_cond_be1': (0.0, 0.576),
     'L0_cond_g2': (1.0, 0.6),
     'L0_cond_be2': (0.0, 0.8),
     'L1_cond_b_proj': (0.0, 0.1),
     'L1_cond_rms_weight': (1.0, 0.2)}
    factors = {'L0_cond_bqkv': 8.0,
     'L0_cond_bproj': 6.496,
     'L0_cond_b1': 8.0,
     'L0_cond_b2': 8.0,
     'L0_cond_bt': 7.254}
    for name, (base, spread) in spreads.items():
        noise = np.random.default_rng([zlib.crc32(name.encode()), seed]).standard_normal(out[name].shape)
        drawn = base * np.exp(spread * noise) if base else spread * noise
        out[name] = jnp.asarray(drawn.astype(out[name].dtype))
    for name, factor in factors.items():
        out[name] = (out[name] * factor).astype(out[name].dtype)
    return out
```

```python
import numpy as np
from contextlib import ExitStack

import concourse.bass as bass
from concourse import mybir


def build_block(nc, t, out):
    fp32 = mybir.dt.float32
    fp32r = mybir.dt.float32r
    ALU = mybir.AluOpType
    ACT = mybir.ActivationFunctionType
    AX = mybir.AxisListType

    class Lane:

        def __init__(self, done):
            self.done, self.count, self.todo, self.waited = done, 0, [], {}

        def put(self, make, after=(), signal=True):
            self.hold(after)
            if signal:
                self.count += 1
                self.todo.append(lambda e: make(e).then_inc(self.done, 1))
            else:
                self.todo.append(make)
            return (self.done, self.count)

        def hold(self, after):
            for sem, value in after:
                if self.waited.get(sem.name, 0) < value:
                    self.waited[sem.name] = value
                    self.todo.append(lambda e, s=sem, v=value: e.wait_ge(s, v))

        def move(self, dst, src, arrival, after=()):
            self.hold(after)
            arrival.value += 16
            dst, src = (v.bitcast(fp32) if v.dtype == fp32r else v for v in (dst, src))
            self.todo.append(lambda e: e.dma_start(dst, src).then_inc(arrival.sem, 16))
            return (arrival.sem, arrival.value)

        def run(self, engine):
            for make in self.todo:
                make(engine)

    class Arrival:

        def __init__(self, sem):
            self.sem, self.value = sem, 0

    class Ring:

        def __init__(self, buffers):
            self.buffers, self.free, self.turn = buffers, [[] for _ in buffers], 0

        def take(self):
            i = self.turn % len(self.buffers)
            self.turn += 1
            return i, self.buffers[i], self.free[i]

    B, L, D = t["x"].shape
    P = 128
    H, HD = 16, 32
    MLP = t["W1"].shape[1]
    KD = D // P
    KM = MLP // P
    CH = 512
    NCH = L // CH
    TT = CH // P
    NG = H * HD // P
    GH = P // HD
    KT = L // P
    LN_EPS, RMS_EPS, Q_EPS = 1e-5, 1e-6, 1e-5
    SCALE = float(HD) ** -0.5
    ROUND = 12582912.0

    whole = ExitStack()
    with whole:
        def sem(name):
            return whole.enter_context(nc.semaphore(name))

        def sb_in(ctx):
            return lambda name, shape, dt=fp32: ctx.enter_context(nc.sbuf_tensor(name, shape, dt))

        keep = sb_in(whole)
        pe, act, dve, pool, sp = (Lane(sem(n)) for n in
                                  ("pe_done", "act_done", "dve_done", "pool_done", "sp_done"))
        lanes = (pe, act, dve, pool, sp)
        arrivals = []

        def arrival(name):
            arrivals.append(Arrival(sem(name)))
            return arrivals[-1]

        def everything():
            return ([(l.done, l.count) for l in lanes if l.count]
                    + [(a.sem, a.value) for a in arrivals if a.value])

        qk_dram = nc.dram_tensor("qk_parts", (B, 2, 2 * D, L), fp32, kind="Internal").ap()
        v_dram = nc.dram_tensor("v_rows", (B, L, D), fp32, kind="Internal").ap()
        x1_dram = nc.dram_tensor("x_after_attention", (B, L, D), fp32, kind="Internal").ap()
        rows_dram = nc.dram_tensor("cond_rows", (6, B, D), fp32, kind="Internal").ap()
        GATE1, GATE1_BIAS, GATE2, GATE2_BIAS, RMS_SCALE, RMS_SHIFT = range(6)

        psum = whole.enter_context(nc.psum_tensor("psum", [P, 8, 512], fp32))
        bank_free = [[] for _ in range(8)]

        ident = keep("ident", [P, P])
        ones = keep("ones", [P, HD])
        cols = keep("cols", [P, 64])
        ln_scale = keep("ln_scale", [P, 2, KD, B])
        ln_shift = keep("ln_shift", [P, 2, KD, B])
        t_z = pool.put(lambda e: e.memset(ident[:, :], 0.0))
        t_ident = pool.put(lambda e: e.affine_select(
            out=ident[:, :], in_=ident[:, :], compare_op=ALU.not_equal, fill=1.0, base=0,
            pattern=[[-1, P]], channel_multiplier=1), after=[t_z])
        t_ones = pool.put(lambda e: e.memset(ones[:, :], 1.0))

        def three_pass(dst, terms, after, signal_last=True):
            parts = []
            for lh, ll, rh, rl in terms:
                parts += [(lh, rh), (lh, rl), (ll, rh)]
            token = None
            for n, (a, b) in enumerate(parts):
                last = n == len(parts) - 1
                token = pe.put(lambda e, a=a, b=b, n=n, last=last: e.matmul(
                    dst, a, b, start=(n == 0), stop=last),
                    after=after if n == 0 else (), signal=last and signal_last)
            return token

        def split_weights(raw, hi, lo, after):
            t_hi = act.put(lambda e: e.activation(hi, raw, ACT.Copy), after=after)
            t_lo = dve.put(lambda e: e.tensor_tensor(lo, raw, hi.bitcast(fp32), ALU.subtract),
                           after=list(after) + [t_hi])
            return [t_hi, t_lo]

        s1 = ExitStack()
        sb = sb_in(s1)
        wqkv_hi = sb("wqkv_hi", [P, KD, 3 * D], fp32r)
        wqkv_lo = sb("wqkv_lo", [P, KD, 3 * D], fp32r)
        x_bufs = [sb(f"x_in{i}", [P, TT, D]) for i in range(2)]
        xn = sb("xn", [P, TT, D])
        h_full = sb("h_full", [P, KD, CH])
        hT = Ring([(sb(f"hT_hi{i}", [P, KD, CH], fp32r), sb(f"hT_lo{i}", [P, KD, CH], fp32r))
                   for i in range(1)])
        qk_out = Ring([sb(f"qk_out{i}", [P, 2, CH], fp32r) for i in range(3)])
        v_out = Ring([sb(f"v_out{i}", [P, D]) for i in range(3)])
        bv = sb("bv", [P, D])
        stats = sb("stats", [P, TT, 6])
        moments = sb("moments", [P, TT, 2])
        inv_std = sb("inv_std", [P, TT])
        a_x = [arrival(f"a_x{i}") for i in range(2)]
        a_qk = [arrival(f"a_qk{i}") for i in range(3)]
        a_v = [arrival(f"a_v{i}") for i in range(3)]
        a_bv = arrival("a_bv")

        s0 = ExitStack()
        sb0 = sb_in(s0)
        wt = sb0("wt", [P, KD, 6 * D])
        wqkv_raw = [sb0(f"wqkv_raw{i}", [P, 3 * D]) for i in range(2)]
        cond = sb0("cond", [B, D])
        silu = sb0("silu", [B, D])
        siluT = sb0("siluT", [P, KD, B])
        vec_rows = sb0("vec_rows", [64, P])
        row_bias = sb0("row_bias", [B, 4, D])
        rows = sb0("rows", [B, 4, D])
        a_cond, a_vec, a_rowb = arrival("a_cond"), arrival("a_vec"), arrival("a_row_bias")
        a_wt = [arrival(f"a_wt{i}") for i in range(2)]
        a_wraw = [arrival(f"a_wraw{i}") for i in range(2)]
        a_rows = arrival("a_rows")

        t_cond = sp.move(cond[:, :], t["cond"], a_cond)
        for name, at, n in (("bt", 0, 24), ("g1", 24, 4), ("be1", 28, 4), ("g2", 32, 4),
                            ("be2", 36, 4), ("bqkv", 40, 8), ("b1", 48, KM)):
            t_vec = sp.move(vec_rows[at:at + n, :],
                            t[name][0:n * P].rearrange("(n p) -> n p", p=P), a_vec)
        BT, G, BE, BQK, B1 = 0, (24, 32), (28, 36), 40, 48
        wt_view = t["Wt"].rearrange("(k p) n -> p k n", p=P)
        t_wt = [sp.move(wt[:, :, i * 3 * D:(i + 1) * 3 * D],
                        wt_view[:, :, i * 3 * D:(i + 1) * 3 * D], a_wt[i]) for i in range(2)]
        x_chunk = [t["x"][b, c * CH:(c + 1) * CH, :].rearrange("(t p) d -> p t d", p=P)
                   for b in range(B) for c in range(NCH)]
        t_x = [None] * len(x_chunk)
        t_x[0] = sp.move(x_bufs[0][:, :, :], x_chunk[0], a_x[0])
        t_wqkv = []
        for k in range(KD):
            raw = wqkv_raw[k % 2]
            t_raw = sp.move(raw[:, :], t["Wqkv"][k * P:(k + 1) * P, :], a_wraw[k % 2],
                            after=t_wqkv[k - 2] if k >= 2 else ())
            t_wqkv.append(split_weights(raw[:, :], wqkv_hi[:, k, :], wqkv_lo[:, k, :], [t_raw]))
        for n, (name, lo) in enumerate((("bt", 2 * D), ("bt", 5 * D), ("bproj", 0), ("b2", 0))):
            t_rowb = sp.move(row_bias[:, n, :], t[name][lo:lo + D].partition_broadcast(B), a_rowb)
        t_bv = sp.move(bv[:, :], t["bqkv"][2 * D:3 * D].partition_broadcast(P), a_bv)

        t_silu = act.put(lambda e: e.activation(silu[:, :], cond[:, :], ACT.Silu), after=[t_cond])
        for k in range(KD):
            t_tr = pe.put(lambda e, k=k: e.transpose(
                psum[:, 0, k * B:(k + 1) * B], silu[:, k * P:(k + 1) * P], ident[0:B, 0:B]),
                after=[t_silu, t_ident])
        t_siluT = dve.put(lambda e: e.tensor_copy(
            siluT[:, :, :], psum[:, 0, 0:KD * B].rearrange("p (k b) -> p k b", k=KD)), after=[t_tr])
        t_tr = pe.put(lambda e: e.transpose(psum[:, 1, 0:64], vec_rows[:, :], ident[0:64, 0:64]),
                      after=[t_vec])
        t_cols = dve.put(lambda e: e.tensor_copy(cols[:, :], psum[:, 1, 0:64]), after=[t_tr])
        for half in range(2):
            bank = 2 + half
            for j in range(2 * KD):
                col = half * 3 * D + j * P
                for k in range(KD):
                    t_mm = pe.put(lambda e, k=k, j=j, col=col, bank=bank: e.matmul(
                        psum[:, bank, j * B:(j + 1) * B], wt[:, k, col:col + P], siluT[:, k, :],
                        start=(k == 0), stop=(k == KD - 1)),
                        after=[t_siluT, t_wt[half]], signal=(k == KD - 1))
            shift, scale = ln_shift[:, half, :, :], ln_scale[:, half, :, :]
            view = psum[:, bank, 0:2 * KD * B].rearrange("p (s k b) -> p s k b", s=2, k=KD)

            def col(at, n=KD):
                return cols[:, at:at + n].unsqueeze(2).to_broadcast([P, n, B])

            bt_at = BT + half * 3 * KD
            t_a = dve.put(lambda e, v=view, o=shift, c=col(bt_at): e.tensor_tensor(
                o, v[:, 0, :, :], c, ALU.add), after=[t_mm, t_cols])
            t_b = dve.put(lambda e, v=view, o=scale, c=col(bt_at + KD): e.tensor_tensor(
                o, v[:, 1, :, :], c, ALU.add), after=[t_mm, t_cols])
            t_b = dve.put(lambda e, o=scale: e.tensor_scalar(o, o, 1.0, None, ALU.add),
                          after=[t_b])
            tmp = sb0(f"ln_tmp{half}", [P, KD, B])
            t_c = dve.put(lambda e, o=tmp, s=scale, c=col(BE[half]): e.tensor_tensor(
                o[:, :, :], s, c, ALU.mult), after=[t_b])
            t_shift = dve.put(lambda e, o=shift, m=tmp: e.tensor_tensor(
                o, o, m[:, :, :], ALU.add), after=[t_a, t_c])
            t_scale = dve.put(lambda e, o=scale, c=col(G[half]): e.tensor_tensor(
                o, o, c, ALU.mult), after=[t_c])
            if half == 0:
                t_ln1 = [t_shift, t_scale]
            else:
                t_ln2 = [t_shift, t_scale]
        for half, (gate, with_bias, bias) in enumerate(((0, 1, 2), (2, 3, 3))):
            bank, at = 4 + half, half * 3 * D + 2 * D
            for k in range(KD):
                t_mm = pe.put(lambda e, k=k, at=at, bank=bank: e.matmul(
                    psum[0:B, bank, :], siluT[:, k, :], wt[:, k, at:at + D],
                    start=(k == 0), stop=(k == KD - 1)),
                    after=[t_siluT, t_wt[half]], signal=(k == KD - 1))
            t_g = dve.put(lambda e, g=gate, h=half, bank=bank: e.tensor_tensor(
                rows[:, g, :], psum[0:B, bank, :], row_bias[:, h, :], ALU.add),
                after=[t_mm, t_rowb])
            t_gb = dve.put(lambda e, g=gate, w=with_bias, bb=2 + half: e.tensor_tensor(
                rows[:, w, :], rows[:, g, :], row_bias[:, bb, :], ALU.mult), after=[t_g])
        t_rows = sp.move(rows_dram[0:4, :, :].rearrange("n b d -> b n d"), rows[:, :, :], a_rows,
                         after=[t_g, t_gb])
        s0_done = everything()
        s0.close()

        sq = ExitStack()
        sbq = sb_in(sq)
        WR = t["w_proj"].shape[0] // P
        wp = sbq("wp", [P, WR, D])
        wq_tmp = [sbq(f"wq_tmp{i}", [P, D]) for i in range(2)]
        wpT = sbq("wpT", [P, KD, WR * P])
        cq = sbq("cq", [B, D])
        cq_tmp = sbq("cq_tmp", [B, D])
        cqT = sbq("cqT", [P, KD, B])
        small = sbq("small", [P, 16])
        ones_sq = sbq("ones_sq", [P, P])
        out_bias = sbq("out_bias", [B, 3, D])
        emb = sbq("emb", [B, 2, D])
        a_wp, a_cq, a_ob = arrival("a_wp"), arrival("a_cq"), arrival("a_out_bias")

        def quantise():
            t_wp = sp.move(wp[:, :, :], t["w_proj"].rearrange("(r p) c -> p r c", p=P), a_wp,
                           after=s0_done)
            t_cq = sp.move(cq[:, :], t["cond"], a_cq, after=s0_done)
            for n, src in enumerate((t["b_proj"][0:D], t["b_proj"][D:2 * D], t["rms_weight"])):
                t_ob = sp.move(out_bias[:, n, :], src.partition_broadcast(B), a_ob)
            t_o = pool.put(lambda e: e.memset(ones_sq[:, :], 1.0), after=s0_done)
            t_abs = dve.put(lambda e: e.tensor_reduce(
                small[:, 0:1], wp[:, :, :], axis=AX.XY, op=ALU.add, apply_absolute_value=True),
                after=[t_wp] + s0_done)
            yield
            bank = 2
            t_sum = pe.put(lambda e: e.matmul(psum[:, bank, 0:1], ones_sq[:, :], small[:, 0:1],
                                              start=True, stop=True),
                           after=[t_o, t_abs] + bank_free[bank])
            t_1 = dve.put(lambda e: e.tensor_scalar(
                small[:, 1:2], psum[:, bank, 0:1], 1.0 / (WR * P * D), Q_EPS, ALU.mult, ALU.max),
                after=[t_sum])
            t_2 = dve.put(lambda e: e.reciprocal(small[:, 2:3], small[:, 1:2]), after=[t_1])
            t_3 = dve.put(lambda e: e.reciprocal(small[:, 3:4], small[:, 2:3]), after=[t_2])
            bank_free[bank] = [t_1]
            yield
            tr_read = [[], []]
            for r in range(WR):
                tmp = wq_tmp[r % 2]
                row = wp[:, r, :]
                t_a = dve.put(lambda e, o=tmp, i=row: e.tensor_scalar(
                    o[:, :], i, small[:, 2:3], ROUND, ALU.mult, ALU.add), after=[t_2])
                t_a = dve.put(lambda e, o=tmp: e.tensor_scalar(
                    o[:, :], o[:, :], ROUND, -1.0, ALU.subtract, ALU.max), after=[t_a])
                t_a = dve.put(lambda e, o=tmp: e.tensor_scalar(
                    o[:, :], o[:, :], 1.0, small[:, 3:4], ALU.min, ALU.mult), after=[t_a, t_3])
                t_a = dve.put(lambda e, o=tmp, i=row: e.tensor_tensor(
                    o[:, :], o[:, :], i, ALU.subtract), after=[t_a])
                t_w = dve.put(lambda e, o=tmp, i=row: e.tensor_tensor(i, i, o[:, :], ALU.add),
                              after=[t_a])
                yield
                for k in range(KD):
                    t_tr = pe.put(lambda e, r=r, k=k: e.transpose(
                        psum[:, bank, k * P:(k + 1) * P], wp[:, r, k * P:(k + 1) * P],
                        ident[:, :]), after=[t_w] + bank_free[bank])
                t_wT = act.put(lambda e, r=r: e.activation(
                    wpT[:, :, r * P:(r + 1) * P],
                    psum[:, bank, :].rearrange("p (k d) -> p k d", k=KD), ACT.Copy),
                    after=[t_tr] + s0_done)
                bank_free[bank] = [t_wT]
            t_m = dve.put(lambda e: e.tensor_reduce(
                small[0:B, 4:5], cq[:, :], axis=AX.X, op=ALU.max, apply_absolute_value=True),
                after=[t_cq])
            t_m = dve.put(lambda e: e.tensor_scalar(
                small[0:B, 5:6], small[0:B, 4:5], Q_EPS, None, ALU.max), after=[t_m])
            t_m = dve.put(lambda e: e.reciprocal(small[0:B, 6:7], small[0:B, 5:6]), after=[t_m])
            t_m = dve.put(lambda e: e.tensor_scalar(
                small[0:B, 7:8], small[0:B, 6:7], 127.0, None, ALU.mult), after=[t_m])
            t_i = dve.put(lambda e: e.reciprocal(small[0:B, 8:9], small[0:B, 7:8]), after=[t_m])
            t_a = dve.put(lambda e: e.tensor_scalar(
                cq_tmp[:, :], cq[:, :], small[0:B, 7:8], ROUND, ALU.mult, ALU.add), after=[t_m])
            t_a = dve.put(lambda e: e.tensor_scalar(
                cq_tmp[:, :], cq_tmp[:, :], ROUND, -128.0, ALU.subtract, ALU.max), after=[t_a])
            t_a = dve.put(lambda e: e.tensor_scalar(
                cq_tmp[:, :], cq_tmp[:, :], 127.0, small[0:B, 8:9], ALU.min, ALU.mult),
                after=[t_a, t_i])
            t_a = dve.put(lambda e: e.tensor_tensor(
                cq_tmp[:, :], cq_tmp[:, :], cq[:, :], ALU.subtract), after=[t_a])
            t_a = dve.put(lambda e: e.tensor_tensor(
                cq[:, :], cq[:, :], cq_tmp[:, :], ALU.add), after=[t_a])
            yield
            for k in range(KD):
                t_tr = pe.put(lambda e, k=k: e.transpose(
                    psum[:, bank, k * B:(k + 1) * B], cq[:, k * P:(k + 1) * P],
                    ident[0:B, 0:B]), after=[t_a] + bank_free[bank])
            t_cqT = dve.put(lambda e: e.tensor_copy(
                cqT[:, :, :], psum[:, bank, 0:KD * B].rearrange("p (k b) -> p k b", k=KD)),
                after=[t_tr])
            bank_free[bank] = [t_cqT]
            yield
            t_emb = []
            for n in range(2):
                for k in range(KD):
                    t_mm = pe.put(lambda e, n=n, k=k: e.matmul(
                        psum[0:B, bank, :], cqT[:, k, :], wpT[:, k, n * D:(n + 1) * D],
                        start=(k == 0), stop=(k == KD - 1)),
                        after=[t_cqT, t_wT] + bank_free[bank], signal=(k == KD - 1))
                t_e = dve.put(lambda e, n=n: e.tensor_tensor(
                    emb[:, n, :], psum[0:B, bank, :], out_bias[:, n, :], ALU.add),
                    after=[t_mm, t_ob])
                bank_free[bank] = [t_e]
                t_emb.append(t_e)
            t_e = dve.put(lambda e: e.scalar_tensor_tensor(
                emb[:, 0, :], emb[:, 0, :], 1.0, out_bias[:, 2, :], ALU.add, ALU.mult),
                after=[t_emb[0]])
            sp.move(rows_dram[4:6, :, :].rearrange("n b d -> b n d"), emb[:, :, :], a_rows,
                    after=[t_e, t_emb[1]])
            yield

        quant = quantise()

        def normalise(x_tile, xn_tile, st, mo, inv, t_in, after, eps=LN_EPS):
            for i in range(TT):
                t_s = dve.put(lambda e, i=i: e.bn_stats(st[:, i, :], x_tile[:, i, :]),
                              after=t_in + after)
            for i in range(TT):
                t_s2 = dve.put(lambda e, i=i: e.bn_aggr(mo[:, i, :], st[:, i, :]), after=[t_s])
            t_v = dve.put(lambda e: e.tensor_scalar(inv[:, :], mo[:, :, 1], eps, None, ALU.add),
                          after=[t_s2])
            t_v = dve.put(lambda e: e.reciprocal(inv[:, :], inv[:, :]), after=[t_v])
            t_q = act.put(lambda e: e.activation(inv[:, :], inv[:, :], ACT.Sqrt), after=[t_v])
            return [dve.put(lambda e, i=i: e.tensor_scalar(
                xn_tile[:, i, :], x_tile[:, i, :], mo[:, i, 0:1], inv[:, i:i + 1],
                ALU.subtract, ALU.mult), after=[t_q] + after) for i in range(TT)]

        n_chunks = B * NCH
        mm_banks = Ring([3, 4, 5, 6, 7])
        tr_banks = Ring([0, 1])
        xn_read = []
        x_read = [[], []]
        h_read = []
        t_xn = normalise(x_bufs[0], xn, stats, moments, inv_std, [t_x[0]], [])
        x_read[0] = t_xn
        for c in range(n_chunks):
            b, half = divmod(c, NCH)
            if c + 1 < n_chunks:
                nxt = (c + 1) % 2
                t_x[c + 1] = sp.move(x_bufs[nxt][:, :, :], x_chunk[c + 1], a_x[nxt],
                                     after=x_read[nxt])
            _, (hi, lo), hT_free = hT.take()
            t_h = []
            xn_read = []
            for f in range(KD):
                i_tr, bank, free = tr_banks.take()
                for i in range(TT):
                    t_tr = pe.put(lambda e, i=i, f=f, bank=bank: e.transpose(
                        psum[:, bank, i * P:(i + 1) * P], xn[:, i, f * P:(f + 1) * P],
                        ident[:, :]), after=t_xn + free + s0_done, signal=(i == TT - 1))
                xn_read.append(t_tr)
                t_f = dve.put(lambda e, f=f, bank=bank, b=b: e.tensor_scalar(
                    h_full[:, f, :], psum[:, bank, :], ln_scale[:, 0, f, b:b + 1],
                    ln_shift[:, 0, f, b:b + 1], ALU.mult, ALU.add),
                    after=[t_tr] + t_ln1 + h_read)
                tr_banks.free[i_tr] = [t_f]
                t_hi = act.put(lambda e, f=f, hi=hi: e.activation(
                    hi[:, f, :], h_full[:, f, :], ACT.Copy), after=[t_f] + hT_free)
                t_lo = dve.put(lambda e, f=f, hi=hi, lo=lo: e.tensor_tensor(
                    lo[:, f, :], h_full[:, f, :], hi[:, f, :].bitcast(fp32), ALU.subtract),
                    after=[t_hi] + hT_free)
                t_h.append([t_hi, t_lo])
            h_read = [t_hi, t_lo]
            hT_last = []
            for j in range(2 * KD):
                i_mm, bank, free = mm_banks.take()
                t_mm = three_pass(psum[:, bank, :], [
                    (wqkv_hi[:, k, j * P:(j + 1) * P], wqkv_lo[:, k, j * P:(j + 1) * P],
                     hi[:, k, :], lo[:, k, :]) for k in range(KD)],
                    after=free + [x for k in t_h for x in k] + [x for k in t_wqkv for x in k])
                i_o, o, o_free = qk_out.take()
                bias = cols[:, BQK + j:BQK + j + 1]
                t_a = act.put(lambda e, o=o, bank=bank, bias=bias: e.activation(
                    o[:, 0, :], psum[:, bank, :], ACT.Identity, bias=bias),
                    after=[t_mm, t_cols] + o_free)
                t_b = dve.put(lambda e, o=o, bank=bank, bias=bias: e.scalar_tensor_tensor(
                    o[:, 1, :], psum[:, bank, :], bias, o[:, 0, :].bitcast(fp32),
                    ALU.add, ALU.subtract), after=[t_a] + o_free)
                mm_banks.free[i_mm] = [t_b]
                t_st = sp.move(qk_dram[b, :, j * P:(j + 1) * P, half * CH:(half + 1) * CH]
                               .rearrange("s p t -> p s t"), o[:, :, :], a_qk[i_o],
                               after=[t_a, t_b])
                qk_out.free[i_o] = [t_st]
                if j == 1 and c + 1 < n_chunks:
                    nxt = (c + 1) % 2
                    t_xn = normalise(x_bufs[nxt], xn, stats, moments, inv_std, [t_x[c + 1]],
                                     xn_read)
                    x_read[nxt] = t_xn
                if c >= 1 and j >= 2:
                    next(quant, None)
            for i in range(TT):
                i_mm, bank, free = mm_banks.take()
                t_mm = three_pass(psum[:, bank, :], [
                    (hi[:, k, i * P:(i + 1) * P], lo[:, k, i * P:(i + 1) * P],
                     wqkv_hi[:, k, 2 * D:3 * D], wqkv_lo[:, k, 2 * D:3 * D]) for k in range(KD)],
                    after=free)
                i_o, o, o_free = v_out.take()
                t_v = dve.put(lambda e, o=o, bank=bank: e.tensor_tensor(
                    o[:, :], psum[:, bank, :], bv[:, :], ALU.add), after=[t_mm, t_bv] + o_free)
                mm_banks.free[i_mm] = [t_v]
                at = half * CH + i * P
                t_st = sp.move(v_dram[b, at:at + P, :], o[:, :], a_v[i_o], after=[t_v])
                v_out.free[i_o] = [t_st]
            hT.free[0] = [t_mm]
        for _ in quant:
            pass
        s1_done = everything()
        sq.close()
        s1.close()

        for lane in lanes:
            lane.hold(s1_done)
        s2 = ExitStack()
        sb = sb_in(s2)
        PARTS = 3 * HD
        ROWS = PARTS + 2
        k_stack = [sb(f"k_stack{i}", [ROWS, GH, L], fp32r) for i in range(2)]
        q_stack = [sb(f"q_stack{i}", [ROWS, GH, CH], fp32r) for i in range(3)]
        v_group = [sb(f"v_group{i}", [P, KT, P]) for i in range(2)]
        probs = [sb(f"probs{i}", [P, GH, 2, CH]) for i in range(3)]
        prob_sum = sb("prob_sum", [P, GH, CH])
        attn = [sb(f"attn{i}", [P, NG, L]) for i in range(2)]
        wproj_hi = sb("wproj_hi", [P, KD, D], fp32r)
        wproj_lo = sb("wproj_lo", [P, KD, D], fp32r)
        attn_hi = sb("attn_hi", [P, NG, P], fp32r)
        attn_lo = sb("attn_lo", [P, NG, P], fp32r)
        x_res = [sb(f"x_res{i}", [P, D]) for i in range(2)]
        x_gated = sb("x_gated", [P, D])
        x1_out = [sb(f"x1_out{i}", [P, D]) for i in range(2)]
        gates = [sb(f"gates{i}", [P, 2, D]) for i in range(2)]
        den_inv = sb("den_inv", [P, CH])
        weighted = [sb(f"weighted{i}", [P, CH]) for i in range(2)]
        max_part = sb("max_part", [P, GH * TT * NCH])
        max_q = sb("max_q", [P, GH * TT])
        negmax_hi = sb("negmax_hi", [GH * TT, P], fp32r)
        negmax_lo = sb("negmax_lo", [GH * TT, P], fp32r)
        a_k = [arrival(f"a_k{i}") for i in range(2)]
        a_q = [arrival(f"a_q{i}") for i in range(3)]
        a_m = [arrival(f"a_m{i}") for i in range(3)]
        a_vg = [arrival(f"a_vg{i}") for i in range(2)]
        a_xr = [arrival(f"a_xr{i}") for i in range(2)]
        a_x1 = [arrival(f"a_x1{i}") for i in range(2)]
        a_g = [arrival(f"a_g{i}") for i in range(2)]
        a_wp2 = arrival("a_wproj")
        SMAX, ST, PV_BANK, DEN_BANK = (0, 1, 2), (3, 4, 5), 6, 7

        t_ones_rows = [dve.put(lambda e, k=k: e.memset(
            k[PARTS:ROWS, :, :].bitcast(fp32), 1.0)) for k in k_stack]

        units = [(b, g, h) for b in range(B) for g in range(NG) for h in range(NCH)]
        NU = len(units)
        PER_B = NG * NCH
        k_free, q_free, vg_free = [[], []], [[], [], []], [[], []]
        t_k, t_q, t_vg, t_m, t_g = {}, {}, {}, {}, {}

        def load_group(G):
            b, g = divmod(G, NG)
            at = D + g * P
            for n, part in enumerate((0, 1, 0)):
                t_k[G] = sp.move(
                    k_stack[G % 2][n * HD:(n + 1) * HD, :, :],
                    qk_dram[b, part, at:at + P, :].rearrange("(h d) t -> d h t", h=GH),
                    a_k[G % 2], after=k_free[G % 2])
            t_vg[G] = sp.move(
                v_group[G % 2][:, :, :],
                v_dram[b, :, g * P:(g + 1) * P].rearrange("(k p) f -> p k f", p=P),
                a_vg[G % 2], after=vg_free[G % 2])

        def load_q(u):
            b, g, h = units[u]
            for n, part in enumerate((0, 0, 1)):
                t_q[u] = sp.move(
                    q_stack[u % 3][n * HD:(n + 1) * HD, :, :],
                    qk_dram[b, part, g * P:(g + 1) * P, h * CH:(h + 1) * CH]
                    .rearrange("(h d) t -> d h t", h=GH),
                    a_q[u % 3], after=q_free[u % 3])

        gates_read = [[], []]

        def load_gates(b):
            for n, kind in enumerate((GATE1, GATE1_BIAS)):
                t_g[b] = sp.move(gates[b % 2][:, n, :], rows_dram[kind, b].partition_broadcast(P),
                                 a_g[b % 2], after=gates_read[b % 2])

        smax_banks = Ring(list(SMAX))
        st_banks = Ring(list(ST))

        def smax_tile(u, n):
            b, g, _ = units[u]
            G = b * NG + g
            h, rest = divmod(n, TT * NCH)
            i, kh = divmod(rest, NCH)
            i_b, bank, free = smax_banks.take()
            q, k = q_stack[u % 3], k_stack[G % 2]
            t_mm = pe.put(lambda e: e.matmul(
                psum[:, bank, :], q[0:PARTS, h, i * P:(i + 1) * P],
                k[0:PARTS, h, kh * CH:(kh + 1) * CH], start=True, stop=True),
                after=free + [t_k[G], t_q[u]])
            t_r = dve.put(lambda e: e.reduce_max(max_part[:, n:n + 1], psum[:, bank, :], AX.X),
                          after=[t_mm] + max_part_read)
            smax_banks.free[i_b] = [t_r]
            return t_r

        max_part_read, negmax_read = [], []

        def send_max(u, t_last):
            t_c = dve.put(lambda e: e.tensor_reduce(
                max_q[:, :], max_part[:, :].rearrange("p (n k) -> p n k", k=NCH), axis=AX.X,
                op=ALU.max), after=[t_last])
            max_part_read[:] = [t_c]
            i_b, bank, free = smax_banks.take()
            t_tr = pe.put(lambda e: e.transpose(psum[0:GH * TT, bank, 0:P], max_q[:, :],
                                                ident[:, :]), after=free + [t_c])
            t_hi = dve.put(lambda e: e.tensor_scalar(
                negmax_hi[:, :], psum[0:GH * TT, bank, 0:P], -1.0, None, ALU.mult),
                after=[t_tr] + negmax_read)
            t_lo = dve.put(lambda e: e.scalar_tensor_tensor(
                negmax_lo[:, :], psum[0:GH * TT, bank, 0:P], -1.0,
                negmax_hi[:, :].bitcast(fp32), ALU.mult, ALU.subtract), after=[t_hi])
            smax_banks.free[i_b] = [t_lo]
            for n, m in enumerate((negmax_hi, negmax_lo)):
                row = q_stack[u % 3][PARTS + n:PARTS + n + 1, :, :]
                t_m[u] = sp.move(row, m[:, :], a_m[u % 3],
                                 after=[t_hi, t_lo] + q_free[u % 3])
            negmax_read[:] = [t_m[u]]

        probs_read = [[], [], []]
        prob_sum_read, attn_hi_read = [], []
        attn_read = [[], []]
        attn_done = {}
        pv_free, den_free = [], []
        x_gated_read = []
        x1_read = [[], []]
        xr_read = [[], []]
        t_xr = {}
        t_wproj = []

        def load_x_res(n):
            b, i = divmod(n, KT)
            t_xr[n] = sp.move(x_res[n % 2][:, :], t["x"][b, i * P:(i + 1) * P, :], a_xr[n % 2],
                              after=xr_read[n % 2])

        def project(n):
            b, i = divmod(n, KT)
            src = attn[b % 2]
            cut = slice(i * P, (i + 1) * P)
            t_hi = act.put(lambda e: e.activation(attn_hi[:, :, :], src[:, :, cut], ACT.Copy),
                           after=attn_done[b] + attn_hi_read)
            t_lo = dve.put(lambda e: e.tensor_tensor(
                attn_lo[:, :, :], src[:, :, cut], attn_hi[:, :, :].bitcast(fp32), ALU.subtract),
                after=[t_hi] + attn_hi_read)
            if i == KT - 1:
                attn_read[b % 2] = [t_hi, t_lo]
            t_xg = pool.put(lambda e: e.tensor_tensor(
                x_gated[:, :], x_res[n % 2][:, :], gates[b % 2][:, 1, :], ALU.add),
                after=[t_xr[n], t_g[b]] + x_gated_read)
            xr_read[n % 2] = [t_xg]

            bank_of = []

            def first_half():
                i_b, bank, free = smax_banks.take()
                bank_of.extend((i_b, bank))
                products(range(KD // 2), free + [t_hi, t_lo] + t_wproj)

            def products(blocks, after):
                for k in blocks:
                    for a, w in ((attn_hi, wproj_hi), (attn_hi, wproj_lo), (attn_lo, wproj_hi)):
                        last = k == KD - 1 and a is attn_lo
                        t_mm = pe.put(lambda e, k=k, a=a, w=w, last=last: e.matmul(
                            psum[:, bank_of[1], :], a[:, k, :], w[:, k, :],
                            start=(k == 0 and a is attn_hi and w is wproj_hi), stop=last),
                            after=after, signal=last)
                return t_mm

            def second_half():
                i_b, bank = bank_of
                t_mm = products(range(KD // 2, KD), ())
                attn_hi_read[:] = [t_mm]
                o = x1_out[n % 2]
                t_y = dve.put(lambda e: e.tensor_tensor(
                    o[:, :], psum[:, bank, :], gates[b % 2][:, 0, :], ALU.mult),
                    after=[t_mm, t_g[b]] + x1_read[n % 2])
                smax_banks.free[i_b] = [t_y]
                t_x1 = dve.put(lambda e: e.tensor_tensor(
                    o[:, :], o[:, :], x_gated[:, :], ALU.add), after=[t_y, t_xg])
                x_gated_read[:] = [t_x1]
                if i == KT - 1:
                    gates_read[b % 2] = [t_x1]
                x1_read[n % 2] = [sp.move(x1_dram[b, i * P:(i + 1) * P, :], o[:, :], a_x1[n % 2],
                                          after=[t_x1])]

            return first_half, second_half

        def slot(u, s):
            return (u * (KT // 2) + s) % len(probs)

        def value_products(u, s, j):
            b, g, _ = units[u]
            G = b * NG + g
            kt = 2 * s + j
            pb = probs[slot(u, s)]
            for h in range(GH):
                t_pv = pe.put(lambda e, h=h: e.matmul(
                    psum[h * HD:(h + 1) * HD, PV_BANK, :],
                    v_group[G % 2][:, kt, h * HD:(h + 1) * HD], pb[:, h, j, :],
                    start=(kt == 0), stop=(kt == KT - 1)),
                    after=(t_p[s] + [t_vg[G]] + pv_free) if h == 0 else (),
                    signal=(h == GH - 1))
            return t_pv

        load_group(0)
        load_q(0)
        if NU > 1:
            load_q(1)
        load_gates(0)
        raw_view = t["Wproj"].rearrange("(k p) n -> p k n", p=P)
        t_raw = sp.move(prob_sum[:, :, :], raw_view, a_wp2)
        t_wproj += split_weights(prob_sum[:, :, :], wproj_hi[:, :, :], wproj_lo[:, :, :],
                                 [t_raw])
        prob_sum_read[:] = t_wproj
        pe.hold(t_ones_rows)
        N_MAX = GH * TT * NCH
        for n in range(N_MAX):
            t_r = smax_tile(0, n)
        send_max(0, t_r)
        STEPS = KT // 2
        SUMMED = STEPS - 1
        LAST = KT // 2 - 1
        PROJ_LAG = PER_B + 1
        t_weighted, t_den = {}, {}
        weighted_read = [[], []]

        def sum_probs(u, s, t_p):
            pb = probs[slot(u, s)]
            if s == 0:
                t_sum = pool.put(lambda e: e.tensor_tensor(
                    prob_sum[:, :, :], pb[:, :, 0, :], pb[:, :, 1, :], ALU.add),
                    after=t_p + prob_sum_read)
            else:
                for j in range(2):
                    t_sum = pool.put(lambda e, j=j: e.tensor_tensor(
                        prob_sum[:, :, :], prob_sum[:, :, :], pb[:, :, j, :], ALU.add),
                        after=t_p + t_summed)
                    t_summed[:] = [t_sum]
            t_summed[:] = [t_sum]

        t_summed = []

        def denominators(u, n, last):
            term = prob_sum[:, :, :] if last else probs[slot(u, LAST)][:, :, n, :]
            for h in range(GH):
                t = pe.put(lambda e, h=h: e.matmul(
                    psum[h * HD:(h + 1) * HD, DEN_BANK, :], ones[:, :], term[:, h, :],
                    start=(n == 0), stop=last),
                    after=(t_summed if last else ()) or [t_ones] + den_free,
                    signal=(h == GH - 1))
            t_den[u] = t
            if last:
                prob_sum_read[:] = [t]
            else:
                probs_read[slot(u, LAST)] = probs_read[slot(u, LAST)] + [t]

        def normalise_attention(u):
            b, g, half = units[u]
            t_i = dve.put(lambda e: e.reciprocal(den_inv[:, :], psum[:, DEN_BANK, :]),
                          after=[t_den[u]])
            den_free[:] = [t_i]
            t_n = dve.put(lambda e: e.tensor_tensor(
                attn[b % 2][:, g, half * CH:(half + 1) * CH], weighted[u % 2][:, :],
                den_inv[:, :], ALU.mult), after=[t_i, t_weighted[u]] + attn_read[b % 2])
            weighted_read[u % 2] = [t_n]
            attn_done[b] = [t_n]

        for u, (b, g, half) in enumerate(units):
            G = b * NG + g
            if half == 0 and (G + 1) * NCH < NU:
                load_group(G + 1)
            if u + 2 < NU:
                load_q(u + 2)
            if u % PER_B == 1 and b >= 1:
                load_gates(b)
            tile = u - PROJ_LAG
            if tile >= 0:
                load_x_res(tile)
            t_p = {}
            max_tokens = []
            for s in range(KT // 2):
                pb = probs[slot(u, s)]
                t_p[s] = []
                if tile >= 0 and s == LAST:
                    first_half, second_half = project(tile)

                def scores(h, s=s, pb=pb):
                    q, k = q_stack[u % 3], k_stack[G % 2]
                    for j in range(2):
                        kt = 2 * s + j
                        i_b, bank, free = st_banks.take()
                        t_mm = pe.put(lambda e, bank=bank, kt=kt: e.matmul(
                            psum[:, bank, :], k[0:ROWS, h, kt * P:(kt + 1) * P],
                            q[0:ROWS, h, :], start=True, stop=True),
                            after=free + [t_m[u], t_q[u], t_k[G]])
                        t_e = act.put(lambda e, bank=bank, j=j: e.activation(
                            pb[:, h, j, :], psum[:, bank, :], ACT.Exp, scale=SCALE),
                            after=[t_mm] + probs_read[slot(u, s)])
                        st_banks.free[i_b] = [t_e]
                    t_p[s].append(t_e)
                    return t_mm

                def maxima():
                    if u + 1 < NU:
                        max_tokens.append(smax_tile(u + 1, len(max_tokens)))

                for pair in range(GH // 2):
                    maxima()
                    t_mm = scores(2 * pair)
                    maxima()
                    if s > 0:
                        t_pv = value_products(u, s - 1, pair)
                    elif u > 0 and pair == 0:
                        denominators(u - 1, 0, False)
                        denominators(u - 1, 1, False)
                    elif u > 0:
                        denominators(u - 1, 2, True)
                    maxima()
                    t_mm = scores(2 * pair + 1)
                    maxima()
                if s > 0:
                    probs_read[slot(u, s - 1)] = [t_pv] + t_summed
                if s < SUMMED:
                    sum_probs(u, s, t_p[s])
            q_free[u % 3] = [t_mm]
            if half == NCH - 1:
                k_free[G % 2] = [t_mm]
            if tile >= 0:
                first_half()
            if u + 1 < NU:
                send_max(u + 1, max_tokens[-1])
            for j in range(2):
                t_pv = value_products(u, LAST, j)
            probs_read[slot(u, LAST)] = [t_pv]
            if half == NCH - 1:
                vg_free[G % 2] = [t_pv]
            t_weighted[u] = act.put(lambda e, u=u: e.activation(
                weighted[u % 2][:, :], psum[:, PV_BANK, :], ACT.Copy),
                after=[t_pv] + weighted_read[u % 2])
            pv_free[:] = [t_weighted[u]]
            if u > 0:
                normalise_attention(u - 1)
            if tile >= 0:
                second_half()
        denominators(NU - 1, 0, False)
        denominators(NU - 1, 1, False)
        denominators(NU - 1, 2, True)
        normalise_attention(NU - 1)
        for tile in range(max(NU - PROJ_LAG, 0), B * KT):
            load_x_res(tile)
            for part in project(tile):
                part()
        s2_done = everything()
        s2.close()

        for lane in lanes:
            lane.hold(s2_done)
        s3 = ExitStack()
        sb = sb_in(s3)
        w1_hi = sb("w1_hi", [P, KD, MLP], fp32r)
        w1_lo = sb("w1_lo", [P, KD, MLP], fp32r)
        w2_hi = sb("w2_hi", [P, KM, D], fp32r)
        w2_lo = sb("w2_lo", [P, KM, D], fp32r)
        sw = ExitStack()
        PIECE = 4 * 512
        w_raw = Ring([sb_in(sw)(f"w_raw{i}", [P, PIECE]) for i in range(4)])
        a_wr = [arrival(f"a_wr{i}") for i in range(4)]
        t_w1, t_w2 = [], []
        for n in range(KM // 4):
            for which in (1, 2):
                i_r, raw, free = w_raw.take()
                if which == 1:
                    src = t["W1"].rearrange("(k p) m -> p k m", p=P)[:, :, n * 512:(n + 1) * 512]
                    cut = (slice(None), slice(None), slice(n * 512, (n + 1) * 512))
                    hi, lo = w1_hi, w1_lo
                else:
                    src = t["W2"].rearrange("(k p) m -> p k m", p=P)[:, 4 * n:4 * n + 4, :]
                    cut = (slice(None), slice(4 * n, 4 * n + 4), slice(None))
                    hi, lo = w2_hi, w2_lo
                view = raw[:, :].rearrange("p (k m) -> p k m", k=4)
                t_r = sp.move(view, src, a_wr[i_r], after=free)
                t_s = split_weights(view, hi[cut], lo[cut], [t_r])
                w_raw.free[i_r] = t_s
                (t_w1 if which == 1 else t_w2).append(t_s)
        sw_done = everything()
        sw.close()
        for lane in lanes:
            lane.hold(sw_done)

        x1 = [sb(f"x1_{i}", [P, TT, D]) for i in range(2)]
        xn_mlp = sb("xn2", [P, TT, D])
        h_hi = sb("h2_hi", [P, KD, CH], fp32r)
        h_lo = sb("h2_lo", [P, KD, CH], fp32r)
        work = Ring([sb(f"work{i}", [P, CH]) for i in range(4)])
        g_parts = Ring([sb(f"g_parts{i}", [P, 2, CH], fp32r) for i in range(3)])
        rows3 = sb("rows3", [P, 4, D])
        y_out = Ring([sb(f"y_out{i}", [P, D]) for i in range(2)])
        stats = sb("stats2", [P, TT, 6])
        moments = sb("moments2", [P, TT, 2])
        inv_std = sb("inv_std2", [P, TT])
        square_sum = sb("square_sum", [P, TT])
        a_x1r = [arrival(f"a_x1r{i}") for i in range(2)]
        a_r3 = arrival("a_rows3")
        a_y = [arrival(f"a_y{i}") for i in range(2)]
        ACC = (0, 1, 2, 3)
        tr_banks = Ring([4, 5])
        up_banks = Ring([6, 7])
        x1_free = [[], []]
        acc_free = [[] for _ in ACC]
        h_free, rows3_free, xn_read = [], [], []
        square_read = []
        t_x1, t_rows3 = {}, {}

        def load_x1(c):
            b, half = divmod(c, NCH)
            t_x1[c] = sp.move(x1[c % 2][:, :, :],
                              x1_dram[b, half * CH:(half + 1) * CH, :]
                              .rearrange("(t p) d -> p t d", p=P), a_x1r[c % 2],
                              after=x1_free[c % 2])

        def load_rows3(b):
            for n in range(4):
                t_rows3[b] = sp.move(rows3[:, n, :],
                                     rows_dram[GATE2 + n, b].partition_broadcast(P), a_r3,
                                     after=rows3_free)

        def add_bias(c):
            b = c // NCH
            return pool.put(lambda e: e.tensor_tensor(
                x1[c % 2][:, :, :], x1[c % 2][:, :, :],
                rows3[:, 1, :].unsqueeze(1).to_broadcast([P, TT, D]), ALU.add),
                after=[t_rows3[b]] + t_norm[c])

        t_norm, t_biased = {}, {}
        lag = []

        def up(c, i):
            i_b, bank, free = up_banks.take()
            t_mm = three_pass(psum[:, bank, :], [
                (w1_hi[:, k, i * P:(i + 1) * P], w1_lo[:, k, i * P:(i + 1) * P],
                 h_hi[:, k, :], h_lo[:, k, :]) for k in range(KD)],
                after=free + t_h + t_w1[i // 4])
            if i == KM - 1:
                h_free[:] = [t_mm]
            i_w, w, w_free = work.take()
            i_g, gp, g_free = g_parts.take()
            bias = cols[:, B1 + i:B1 + i + 1]
            t_f = act.put(lambda e: e.activation(w[:, :], psum[:, bank, :], ACT.Gelu, bias=bias),
                          after=[t_mm] + w_free)
            t_hi = act.put(lambda e: e.activation(gp[:, 0, :], psum[:, bank, :], ACT.Gelu,
                                                  bias=bias), after=g_free)
            up_banks.free[i_b] = [t_hi]
            t_lo = dve.put(lambda e: e.tensor_tensor(
                gp[:, 1, :], w[:, :], gp[:, 0, :].bitcast(fp32), ALU.subtract),
                after=[t_f, t_hi] + g_free)
            work.free[i_w] = [t_lo]

            def down():
                for n in range(TT):
                    cut = slice(n * P, (n + 1) * P)
                    pairs = ((0, w2_hi), (0, w2_lo), (1, w2_hi))
                    for m, (part, w2) in enumerate(pairs):
                        last = i == KM - 1 and m == 2
                        t_d = pe.put(lambda e, n=n, cut=cut, part=part, w2=w2, m=m, last=last:
                                     e.matmul(psum[:, ACC[n], :], gp[:, part, cut],
                                              w2[:, i, :], start=(i == 0 and m == 0),
                                              stop=last),
                                     after=([t_hi, t_lo] + t_w2[i // 4]
                                            + (acc_free[n] if i == 0 else [])) if m == 0 else (),
                                     signal=m == 2)
                    t_down[n] = t_d
                g_parts.free[i_g] = [t_d]

            return down

        t_down = [None] * TT

        def finish_first(c):
            b = c // NCH
            t_x2 = []
            for n in range(TT):
                i_w, w, w_free = work.take()
                t_y = dve.put(lambda e, n=n, w=w: e.tensor_tensor(
                    w[:, :], psum[:, ACC[n], :], rows3[:, 0, :], ALU.mult),
                    after=[t_down[n], t_rows3[b]] + w_free)
                acc_free[n] = [t_y]
                t_x2.append(dve.put(lambda e, n=n, w=w: e.tensor_tensor(
                    x1[c % 2][:, n, :], x1[c % 2][:, n, :], w[:, :], ALU.add),
                    after=[t_y, t_biased[c]]))
                work.free[i_w] = [t_x2[-1]]
            return t_x2

        def finish_second(c, t_x2):
            for n in range(TT):
                i_w, w, w_free = work.take()
                t_s = act.put(lambda e, n=n, w=w: e.activation(
                    w[:, :], x1[c % 2][:, n, :], ACT.Square,
                    accum_out=square_sum[:, n:n + 1]), after=[t_x2[n]] + w_free + square_read)
                work.free[i_w] = [t_s]
            t_r = dve.put(lambda e: e.tensor_scalar(
                square_sum[:, :], square_sum[:, :], 1.0 / D, RMS_EPS, ALU.mult, ALU.add),
                after=[t_s])
            t_r = dve.put(lambda e: e.reciprocal(square_sum[:, :], square_sum[:, :]),
                          after=[t_r])
            return act.put(lambda e: e.activation(square_sum[:, :], square_sum[:, :], ACT.Sqrt),
                           after=[t_r])

        def finish_third(c, t_r, n):
            b, half = divmod(c, NCH)
            i_y, y, y_free = y_out.take()
            t_a = dve.put(lambda e: e.scalar_tensor_tensor(
                y[:, :], x1[c % 2][:, n, :], square_sum[:, n:n + 1], rows3[:, 2, :],
                ALU.mult, ALU.mult), after=[t_r, t_rows3[b]] + y_free)
            t_b = pool.put(lambda e: e.tensor_tensor(y[:, :], y[:, :], rows3[:, 3, :], ALU.add),
                           after=[t_a])
            at = half * CH + n * P
            t_st = sp.move(out[b, at:at + P, :], y[:, :], a_y[i_y], after=[t_b])
            y_out.free[i_y] = [t_st]
            if n == TT - 1:
                square_read[:] = [t_a]
                x1_free[c % 2] = [t_a]
                rows3_free[:] = [t_b]

        load_x1(0)
        load_rows3(0)
        t_norm[0] = normalise(x1[0], xn_mlp, stats, moments, inv_std, [t_x1[0]], [])
        for c in range(n_chunks + 1):
            b, half = divmod(c, NCH)
            live = c < n_chunks
            if live:
                t_h = []
                xn_read = []
                for f in range(KD):
                    i_tr, bank, free = tr_banks.take()
                    for i in range(TT):
                        t_tr = pe.put(lambda e, i=i, f=f, bank=bank: e.transpose(
                            psum[:, bank, i * P:(i + 1) * P], xn_mlp[:, i, f * P:(f + 1) * P],
                            ident[:, :]), after=t_norm[c] + free, signal=(i == TT - 1))
                    xn_read.append(t_tr)
                    i_w, w, w_free = work.take()
                    t_f = dve.put(lambda e, f=f, bank=bank, b=b, w=w: e.tensor_scalar(
                        w[:, :], psum[:, bank, :], ln_scale[:, 1, f, b:b + 1],
                        ln_shift[:, 1, f, b:b + 1], ALU.mult, ALU.add),
                        after=[t_tr] + t_ln2 + w_free)
                    tr_banks.free[i_tr] = [t_f]
                    t_hi = act.put(lambda e, f=f, w=w: e.activation(
                        h_hi[:, f, :], w[:, :], ACT.Copy), after=[t_f] + h_free)
                    t_lo = dve.put(lambda e, f=f, w=w: e.tensor_tensor(
                        h_lo[:, f, :], w[:, :], h_hi[:, f, :].bitcast(fp32), ALU.subtract),
                        after=[t_hi] + h_free)
                    work.free[i_w] = [t_lo]
                    t_h += [t_hi, t_lo]
            for down in lag:
                down()
            lag = []
            if c >= 1:
                t_x2 = finish_first(c - 1)
            if live:
                for i in range(KM):
                    lag.append(up(c, i))
                    if len(lag) > 2:
                        lag.pop(0)()
                    if c >= 1 and i == 2:
                        t_r = finish_second(c - 1, t_x2)
                    if c >= 1 and 3 <= i < 3 + TT:
                        finish_third(c - 1, t_r, i - 3)
                    if i == 7 and c + 1 < n_chunks:
                        load_x1(c + 1)
                    if i == 8 and c > 0 and half == 0:
                        load_rows3(b)
                    if i == 9:
                        t_biased[c] = add_bias(c)
                    if i == 10 and c + 1 < n_chunks:
                        t_norm[c + 1] = normalise(x1[(c + 1) % 2], xn_mlp, stats, moments, inv_std,
                                                  [t_x1[c + 1]], xn_read)
            else:
                t_r = finish_second(c - 1, t_x2)
                for n in range(TT):
                    finish_third(c - 1, t_r, n)
        s3.close()

        block = whole.enter_context(nc.Block())
        final = [(a.sem, a.value) for a in arrivals if a.value]
        for s_, v_ in final:
            sp.todo.append(lambda e, s_=s_, v_=v_: e.wait_ge(s_, v_))

        @block.sync
        def _(engine):
            sp.run(engine)

        @block.scalar
        def _(engine):
            act.run(engine)

        @block.vector
        def _(engine):
            dve.run(engine)

        @block.gpsimd
        def _(engine):
            pool.run(engine)

        @block.tensor
        def _(engine):
            pe.run(engine)


_SHORT = {"cond_1024": "cond"}


def kernel(**inputs):
    import concourse.bacc as bacc
    from concourse.bass_utils import run_bass_kernel_spmd

    nc = bacc.Bacc("TRN2", target_bir_lowering=False, num_devices=1)
    arrays, tensors = {}, {}
    for name, a in inputs.items():
        short = _SHORT.get(name, name.replace("L0_cond_", "").replace("L1_cond_", ""))
        a = np.ascontiguousarray(a)
        arrays[f"in_{short}"] = a
        tensors[short] = nc.dram_tensor(f"in_{short}", a.shape, mybir.dt.from_np(a.dtype),
                                        kind="ExternalInput").ap()
    x = arrays["in_x"]
    out = nc.dram_tensor("out_0", x.shape, mybir.dt.from_np(x.dtype), kind="ExternalOutput").ap()
    build_block(nc, tensors, out)
    result = run_bass_kernel_spmd(nc, [arrays], core_ids=[0])
    return result.results[0]["out_0"]
```

```python
import numpy as np
from contextlib import ExitStack

import concourse.bass as bass
from concourse import mybir


def build_block(nc, t, out):
    fp32 = mybir.dt.float32
    fp32r = mybir.dt.float32r
    ALU = mybir.AluOpType
    ACT = mybir.ActivationFunctionType
    AX = mybir.AxisListType

    class Lane:

        def __init__(self, done):
            self.done, self.count, self.todo, self.waited = done, 0, [], {}

        def put(self, make, after=(), signal=True):
            self.hold(after)
            if signal:
                self.count += 1
                self.todo.append(lambda e: make(e).then_inc(self.done, 1))
            else:
                self.todo.append(make)
            return (self.done, self.count)

        def hold(self, after):
            for sem, value in after:
                if self.waited.get(sem.name, 0) < value:
                    self.waited[sem.name] = value
                    self.todo.append(lambda e, s=sem, v=value: e.wait_ge(s, v))

        def move(self, dst, src, arrival, after=()):
            self.hold(after)
            arrival.value += 16
            dst, src = (v.bitcast(fp32) if v.dtype == fp32r else v for v in (dst, src))
            self.todo.append(lambda e: e.dma_start(dst, src).then_inc(arrival.sem, 16))
            return (arrival.sem, arrival.value)

        def run(self, engine):
            for make in self.todo:
                make(engine)

    class Arrival:

        def __init__(self, sem):
            self.sem, self.value = sem, 0

    class Ring:

        def __init__(self, buffers):
            self.buffers, self.free, self.turn = buffers, [[] for _ in buffers], 0

        def take(self):
            i = self.turn % len(self.buffers)
            self.turn += 1
            return i, self.buffers[i], self.free[i]

    B, L, D = t["x"].shape
    P = 128
    H, HD = 16, 32
    MLP = t["W1"].shape[1]
    KD = D // P
    KM = MLP // P
    CH = 512
    NCH = L // CH
    TT = CH // P
    NG = H * HD // P
    GH = P // HD
    KT = L // P
    LN_EPS, RMS_EPS, Q_EPS = 1e-5, 1e-6, 1e-5
    SCALE = float(HD) ** -0.5
    ROUND = 12582912.0

    whole = ExitStack()
    with whole:
        def sem(name):
            return whole.enter_context(nc.semaphore(name))

        ALIGN = 32
        holes = [[(nc.sbuf_base + ALIGN - 1) // ALIGN * ALIGN, nc.sbuf_top // ALIGN * ALIGN]]

        def place(name, shape, dt=fp32, top=False):
            size = -(-int(np.prod(shape[1:])) * 4 // ALIGN) * ALIGN
            fits = [x for x in holes if x[1] - x[0] >= size]
            assert fits, f"no room for {name}: {size} bytes, holes {holes}"
            if top:
                fits[-1][1] -= size
                at = fits[-1][1]
            else:
                at = fits[0][0]
                fits[0][0] += size
            return nc.alloc_sbuf_tensor_at(name, shape, dt, offset=at), (at, at + size)

        def give_back(ranges):
            cuts = sorted([list(x) for x in ranges] + [x for x in holes if x[0] < x[1]])
            holes[:] = []
            for lo, hi in cuts:
                if holes and holes[-1][1] == lo:
                    holes[-1][1] = hi
                else:
                    holes.append([lo, hi])

        class Region:

            def __init__(self, top=False):
                self.ranges, self.top = [], top

            def __call__(self, name, shape, dt=fp32):
                view, span = place(name, shape, dt, self.top)
                self.ranges.append(span)
                return view

            def close(self):
                give_back(self.ranges)
                self.ranges = []

        keep = Region()
        pe, act, dve, pool, sp = (Lane(sem(n)) for n in
                                  ("pe_done", "act_done", "dve_done", "pool_done", "sp_done"))
        lanes = (pe, act, dve, pool, sp)
        arrivals = []

        def arrival(name):
            arrivals.append(Arrival(sem(name)))
            return arrivals[-1]

        def everything():
            return ([(l.done, l.count) for l in lanes if l.count]
                    + [(a.sem, a.value) for a in arrivals if a.value])

        qk_dram = nc.dram_tensor("qk_parts", (B, 2, 2 * D, L), fp32, kind="Internal").ap()
        v_dram = nc.dram_tensor("v_rows", (B, L, D), fp32, kind="Internal").ap()
        x1_dram = nc.dram_tensor("x_after_attention", (B, L, D), fp32, kind="Internal").ap()
        rows_dram = nc.dram_tensor("cond_rows", (6, B, D), fp32, kind="Internal").ap()
        GATE1, GATE1_BIAS, GATE2, GATE2_BIAS, RMS_SCALE, RMS_SHIFT = range(6)

        psum = whole.enter_context(nc.psum_tensor("psum", [P, 8, 512], fp32))
        bank_free = [[] for _ in range(8)]

        ident = keep("ident", [P, P])
        ones = keep("ones", [P, HD])
        cols = keep("cols", [P, 64])
        ln_scale = keep("ln_scale", [P, 2, KD, B])
        ln_shift = keep("ln_shift", [P, 2, KD, B])
        t_z = pool.put(lambda e: e.memset(ident[:, :], 0.0))
        t_ident = pool.put(lambda e: e.affine_select(
            out=ident[:, :], in_=ident[:, :], compare_op=ALU.not_equal, fill=1.0, base=0,
            pattern=[[-1, P]], channel_multiplier=1), after=[t_z])
        t_ones = pool.put(lambda e: e.memset(ones[:, :], 1.0))

        def three_pass(dst, terms, after, between=None):
            parts = []
            for lh, ll, rh, rl in terms:
                parts += [(lh, rh), (lh, rl), (ll, rh)]
            token = None
            for n, (a, b) in enumerate(parts):
                last = n == len(parts) - 1
                if between and n % 3 == 0:
                    between()
                token = pe.put(lambda e, a=a, b=b, n=n, last=last: e.matmul(
                    dst, a, b, start=(n == 0), stop=last),
                    after=after if n == 0 else (), signal=last)
            return token

        def split_weights(raw, hi, lo, after, subtract=None):
            t_hi = act.put(lambda e: e.activation(hi, raw, ACT.Copy), after=after)
            t_lo = (subtract or dve).put(lambda e: e.tensor_tensor(lo, raw, hi.bitcast(fp32), ALU.subtract),
                           after=list(after) + [t_hi])
            return [t_hi, t_lo]

        s1 = sb = Region()
        wqkv_hi = sb("wqkv_hi", [P, KD, 3 * D], fp32r)
        wqkv_lo = sb("wqkv_lo", [P, KD, 3 * D], fp32r)
        x_bufs = [sb(f"x_in{i}", [P, TT, D]) for i in range(2)]
        xn = sb("xn", [P, TT, D])
        h_full = Ring([sb(f"h_full{i}", [P, CH]) for i in range(2)])
        hT = Ring([(sb(f"hT_hi{i}", [P, KD, CH], fp32r), sb(f"hT_lo{i}", [P, KD, CH], fp32r))
                   for i in range(2)])
        qk_out = Ring([sb(f"qk_out{i}", [P, 2, CH], fp32r) for i in range(3)])
        v_out = Ring([sb(f"v_out{i}", [P, D]) for i in range(3)])
        bv = sb("bv", [P, D])
        stats = sb("stats", [P, TT, 6])
        moments = sb("moments", [P, TT, 2])
        inv_std = sb("inv_std", [P, TT])
        a_x = [arrival(f"a_x{i}") for i in range(2)]
        a_qk = [arrival(f"a_qk{i}") for i in range(3)]
        a_v = [arrival(f"a_v{i}") for i in range(3)]
        a_bv = arrival("a_bv")
        n_chunks = B * NCH
        SIDE_BANK = 2
        mm_banks = Ring([3, 4, 5, 6, 7])
        tr_banks = Ring([0, 1])

        s0 = sb0 = Region()
        wt = [sb0(f"wt{i}", [P, KD, 3 * D]) for i in range(2)]
        RAW = 3 * D // 2
        wqkv_raw = Ring([sb0(f"wqkv_raw{i}", [P, RAW]) for i in range(KD)])
        cond = sb0("cond", [B, D])
        silu = sb0("silu", [B, D])
        siluT = sb0("siluT", [P, KD, B])
        vec_rows = sb0("vec_rows", [64, P])
        row_bias = sb0("row_bias", [B, 2, D])
        rows = sb0("rows", [B, 2, D])
        ln_tmp = [sb0(f"ln_tmp{i}", [P, KD, B]) for i in range(2)]
        a_cond, a_vec, a_rowb = arrival("a_cond"), arrival("a_vec"), arrival("a_row_bias")
        a_wt = [arrival(f"a_wt{i}") for i in range(2)]
        a_wtg = arrival("a_wt_gate")
        a_wraw = [arrival(f"a_wraw{i}") for i in range(KD)]
        a_rows = arrival("a_rows")

        wt_view = t["Wt"].rearrange("(k p) n -> p k n", p=P)
        x_chunk = [t["x"][b, c * CH:(c + 1) * CH, :].rearrange("(t p) d -> p t d", p=P)
                   for b in range(B) for c in range(NCH)]
        t_x = [None] * len(x_chunk)
        t_cond = sp.move(cond[:, :], t["cond"], a_cond)
        t_x[0] = sp.move(x_bufs[0][:, :, :], x_chunk[0], a_x[0])
        for name, at, n in (("bt", 0, 24), ("g1", 24, 4), ("be1", 28, 4), ("g2", 32, 4),
                            ("be2", 36, 4), ("bqkv", 40, 8), ("b1", 48, KM)):
            t_vec = sp.move(vec_rows[at:at + n, :],
                            t[name][0:n * P].rearrange("(n p) -> n p", p=P), a_vec)
        BT, GAMMA, BETA, BQK, B1 = 0, (24, 32), (28, 36), 40, 48
        t_wt = [[sp.move(wt[0][:, :, 0:2 * D], wt_view[:, :, 0:2 * D], a_wt[0])], None]
        t_wqkv = [[], []]

        def load_wqkv(n):
            loads = []
            for k in range(KD):
                i_r, raw, free = wqkv_raw.take()
                loads.append(sp.move(raw[:, :], t["Wqkv"][k * P:(k + 1) * P,
                                                          n * RAW:(n + 1) * RAW],
                                     a_wraw[i_r], after=free))
            return loads

        def split_wqkv(n, loads):
            cut = slice(n * RAW, (n + 1) * RAW)
            for k in range(KD):
                t_s = split_weights(wqkv_raw.buffers[k][:, :], wqkv_hi[:, k, cut],
                                    wqkv_lo[:, k, cut], [loads[k]])
                wqkv_raw.free[k] = t_s
                t_wqkv[n] += t_s

        wqkv_loads = load_wqkv(0)

        t_silu = act.put(lambda e: e.activation(silu[:, :], cond[:, :], ACT.Silu), after=[t_cond])
        for k in range(KD):
            t_tr = pe.put(lambda e, k=k: e.transpose(
                psum[:, mm_banks.buffers[0], k * B:(k + 1) * B], silu[:, k * P:(k + 1) * P],
                ident[0:B, 0:B]), after=[t_silu, t_ident])
        t_siluT = dve.put(lambda e: e.tensor_copy(
            siluT[:, :, :], psum[:, mm_banks.buffers[0], 0:KD * B]
            .rearrange("p (k b) -> p k b", k=KD)), after=[t_tr])
        mm_banks.free[0] = [t_siluT]
        t_tr = pe.put(lambda e: e.transpose(psum[:, mm_banks.buffers[1], 0:64], vec_rows[:, :],
                                            ident[0:64, 0:64]), after=[t_vec])
        t_cols = dve.put(lambda e: e.tensor_copy(cols[:, :], psum[:, mm_banks.buffers[1], 0:64]),
                         after=[t_tr])
        mm_banks.free[1] = [t_cols]

        def norm_vectors(half):
            bank = SIDE_BANK
            for j in range(2 * KD):
                for k in range(KD):
                    t_mm = pe.put(lambda e, k=k, j=j: e.matmul(
                        psum[:, bank, j * B:(j + 1) * B], wt[half][:, k, j * P:(j + 1) * P],
                        siluT[:, k, :], start=(k == 0), stop=(k == KD - 1)),
                        after=[t_siluT] + t_wt[half] + bank_free[bank], signal=(k == KD - 1))
            shift, scale = ln_shift[:, half, :, :], ln_scale[:, half, :, :]
            view = psum[:, bank, 0:2 * KD * B].rearrange("p (s k b) -> p s k b", s=2, k=KD)

            def col(at):
                return cols[:, at:at + KD].unsqueeze(2).to_broadcast([P, KD, B])

            bt_at = BT + half * 3 * KD
            t_a = dve.put(lambda e: e.tensor_tensor(shift, view[:, 0, :, :], col(bt_at), ALU.add),
                          after=[t_mm, t_cols])
            t_b = dve.put(lambda e: e.scalar_tensor_tensor(
                scale, view[:, 1, :, :], 1.0, col(bt_at + KD), ALU.add, ALU.add),
                after=[t_mm, t_cols])
            bank_free[bank] = [t_b]
            tmp = ln_tmp[half]
            t_c = dve.put(lambda e: e.tensor_tensor(tmp[:, :, :], scale, col(BETA[half]), ALU.mult),
                          after=[t_b])
            t_shift = dve.put(lambda e: e.tensor_tensor(shift, shift, tmp[:, :, :], ALU.add),
                              after=[t_a, t_c])
            t_scale = dve.put(lambda e: e.tensor_tensor(scale, scale, col(GAMMA[half]), ALU.mult),
                              after=[t_c])
            return [t_shift, t_scale]

        t_ln1 = norm_vectors(0)
        t_ln2 = []
        s0_done, side_done = [], []

        def condition():
            yield
            t_ln2.extend(norm_vectors(1))
            yield
            t_rows = []
            for half, (bt_at, bias) in enumerate(((2 * D, "bproj"), (5 * D, "b2"))):
                bank = SIDE_BANK
                for n, src in enumerate((t["bt"][bt_at:bt_at + D], t[bias][0:D])):
                    t_rowb = sp.move(row_bias[:, n, :], src.partition_broadcast(B), a_rowb,
                                     after=t_rows)
                for k in range(KD):
                    t_mm = pe.put(lambda e, k=k, half=half: e.matmul(
                        psum[0:B, bank, :], siluT[:, k, :], wt[half][:, k, 2 * D:3 * D],
                        start=(k == 0), stop=(k == KD - 1)),
                        after=[t_siluT, t_wt_gate] + t_wt[1] + bank_free[bank],
                        signal=(k == KD - 1))
                t_g = dve.put(lambda e: e.tensor_tensor(
                    rows[:, 0, :], psum[0:B, bank, :], row_bias[:, 0, :], ALU.add),
                    after=[t_mm, t_rowb] + t_rows)
                bank_free[bank] = [t_g]
                t_gb = dve.put(lambda e: e.tensor_tensor(
                    rows[:, 1, :], rows[:, 0, :], row_bias[:, 1, :], ALU.mult), after=[t_g])
                t_rows = [sp.move(
                    rows_dram[2 * half:2 * half + 2, :, :].rearrange("n b d -> b n d"),
                    rows[:, :, :], a_rows, after=[t_g, t_gb])]
                yield
            s0_done.extend(everything())
            yield

        side_work = [condition()]

        def next_side():
            while side_work and next(side_work[0], "end") == "end":
                side_work.pop(0)

        WR = t["w_proj"].shape[0] // P
        sq = sbq = Region()
        a_wp, a_cq, a_ob = arrival("a_wp"), arrival("a_cq"), arrival("a_out_bias")

        def quantise():
            s0.close()
            wp = sbq("wp", [P, WR, D])
            wq_tmp = [sbq(f"wq_tmp{i}", [P, D]) for i in range(2)]
            wpT = sbq("wpT", [P, KD, WR * P])
            cq = sbq("cq", [B, D])
            cq_tmp = sbq("cq_tmp", [B, D])
            cqT = sbq("cqT", [P, KD, B])
            small = sbq("small", [P, 16])
            ones_sq = sbq("ones_sq", [P, P])
            out_bias = sbq("out_bias", [B, 3, D])
            emb = sbq("emb", [B, 2, D])
            t_emb = []
            t_wp = sp.move(wp[:, :, :], t["w_proj"].rearrange("(r p) c -> p r c", p=P), a_wp,
                           after=s0_done)
            t_cq = sp.move(cq[:, :], t["cond"], a_cq, after=s0_done)
            for n, src in enumerate((t["b_proj"][0:D], t["b_proj"][D:2 * D], t["rms_weight"])):
                t_ob = sp.move(out_bias[:, n, :], src.partition_broadcast(B), a_ob)
            t_o = pool.put(lambda e: e.memset(ones_sq[:, :], 1.0), after=s0_done)
            for r in range(WR):
                t_abs = dve.put(lambda e, r=r: e.tensor_reduce(
                    small[:, 8 + r:9 + r], wp[:, r, :], axis=AX.X, op=ALU.add,
                    apply_absolute_value=True), after=[t_wp] + s0_done)
                if r % 2:
                    yield
            t_abs = dve.put(lambda e: e.reduce_sum(small[:, 0:1], small[:, 8:8 + WR], AX.X),
                            after=[t_abs])
            yield
            yield
            bank = SIDE_BANK
            t_sum = pe.put(lambda e: e.matmul(psum[:, bank, 0:1], ones_sq[:, :], small[:, 0:1],
                                              start=True, stop=True),
                           after=[t_o, t_abs] + bank_free[bank])
            t_1 = dve.put(lambda e: e.tensor_scalar(
                small[:, 1:2], psum[:, bank, 0:1], 1.0 / (WR * P * D), Q_EPS, ALU.mult, ALU.max),
                after=[t_sum])
            t_2 = dve.put(lambda e: e.reciprocal(small[:, 2:3], small[:, 1:2]), after=[t_1])
            t_3 = dve.put(lambda e: e.reciprocal(small[:, 3:4], small[:, 2:3]), after=[t_2])
            bank_free[bank] = [t_1]
            yield
            tr_read = [[], []]
            for r in range(WR):
                tmp = wq_tmp[r % 2]
                row = wp[:, r, :]
                t_a = dve.put(lambda e, o=tmp, i=row: e.tensor_scalar(
                    o[:, :], i, small[:, 2:3], ROUND, ALU.mult, ALU.add), after=[t_2])
                t_a = dve.put(lambda e, o=tmp: e.tensor_scalar(
                    o[:, :], o[:, :], ROUND, -1.0, ALU.subtract, ALU.max), after=[t_a])
                t_a = dve.put(lambda e, o=tmp: e.tensor_scalar(
                    o[:, :], o[:, :], 1.0, small[:, 3:4], ALU.min, ALU.mult), after=[t_a, t_3])
                t_a = dve.put(lambda e, o=tmp, i=row: e.tensor_tensor(
                    o[:, :], o[:, :], i, ALU.subtract), after=[t_a])
                t_w = dve.put(lambda e, o=tmp, i=row: e.tensor_tensor(i, i, o[:, :], ALU.add),
                              after=[t_a])
                yield
                yield
                yield
                for k in range(KD):
                    t_tr = pe.put(lambda e, r=r, k=k: e.transpose(
                        psum[:, bank, k * P:(k + 1) * P], wp[:, r, k * P:(k + 1) * P],
                        ident[:, :]), after=[t_w] + bank_free[bank])
                t_wT = act.put(lambda e, r=r: e.activation(
                    wpT[:, :, r * P:(r + 1) * P],
                    psum[:, bank, :].rearrange("p (k d) -> p k d", k=KD), ACT.Copy),
                    after=[t_tr] + s0_done)
                bank_free[bank] = [t_wT]
            t_m = dve.put(lambda e: e.tensor_reduce(
                small[0:B, 4:5], cq[:, :], axis=AX.X, op=ALU.max, apply_absolute_value=True),
                after=[t_cq])
            t_m = dve.put(lambda e: e.tensor_scalar(
                small[0:B, 5:6], small[0:B, 4:5], Q_EPS, None, ALU.max), after=[t_m])
            t_m = dve.put(lambda e: e.reciprocal(small[0:B, 6:7], small[0:B, 5:6]), after=[t_m])
            t_m = dve.put(lambda e: e.tensor_scalar(
                small[0:B, 7:8], small[0:B, 6:7], 127.0, None, ALU.mult), after=[t_m])
            t_i = dve.put(lambda e: e.reciprocal(small[0:B, 8:9], small[0:B, 7:8]), after=[t_m])
            t_a = dve.put(lambda e: e.tensor_scalar(
                cq_tmp[:, :], cq[:, :], small[0:B, 7:8], ROUND, ALU.mult, ALU.add), after=[t_m])
            t_a = dve.put(lambda e: e.tensor_scalar(
                cq_tmp[:, :], cq_tmp[:, :], ROUND, -128.0, ALU.subtract, ALU.max), after=[t_a])
            t_a = dve.put(lambda e: e.tensor_scalar(
                cq_tmp[:, :], cq_tmp[:, :], 127.0, small[0:B, 8:9], ALU.min, ALU.mult),
                after=[t_a, t_i])
            t_a = dve.put(lambda e: e.tensor_tensor(
                cq_tmp[:, :], cq_tmp[:, :], cq[:, :], ALU.subtract), after=[t_a])
            t_a = dve.put(lambda e: e.tensor_tensor(
                cq[:, :], cq[:, :], cq_tmp[:, :], ALU.add), after=[t_a])
            yield
            yield
            yield
            for k in range(KD):
                t_tr = pe.put(lambda e, k=k: e.transpose(
                    psum[:, bank, k * B:(k + 1) * B], cq[:, k * P:(k + 1) * P],
                    ident[0:B, 0:B]), after=[t_a] + bank_free[bank])
            t_cqT = dve.put(lambda e: e.tensor_copy(
                cqT[:, :, :], psum[:, bank, 0:KD * B].rearrange("p (k b) -> p k b", k=KD)),
                after=[t_tr])
            bank_free[bank] = [t_cqT]
            yield
            for n in range(2):
                for k in range(KD):
                    t_mm = pe.put(lambda e, n=n, k=k: e.matmul(
                        psum[0:B, bank, :], cqT[:, k, :], wpT[:, k, n * D:(n + 1) * D],
                        start=(k == 0), stop=(k == KD - 1)),
                        after=[t_cqT, t_wT] + bank_free[bank], signal=(k == KD - 1))
                t_e = dve.put(lambda e, n=n: e.tensor_tensor(
                    emb[:, n, :], psum[0:B, bank, :], out_bias[:, n, :], ALU.add),
                    after=[t_mm, t_ob])
                bank_free[bank] = [t_e]
                t_emb.append(t_e)
            t_e = dve.put(lambda e: e.scalar_tensor_tensor(
                emb[:, 0, :], emb[:, 0, :], 1.0, out_bias[:, 2, :], ALU.add, ALU.mult),
                after=[t_emb[0]])
            sp.move(rows_dram[4:6, :, :].rearrange("n b d -> b n d"), emb[:, :, :], a_rows,
                    after=[t_e, t_emb[1]])
            side_done.extend(everything())
            sq.close()
            yield

        side_work.append(quantise())

        def normalise(x_tile, xn_tile, st, mo, inv, t_in, after, eps=LN_EPS):
            for i in range(TT):
                t_s = dve.put(lambda e, i=i: e.bn_stats(st[:, i, :], x_tile[:, i, :]),
                              after=t_in + after)
            for i in range(TT):
                t_s2 = dve.put(lambda e, i=i: e.bn_aggr(mo[:, i, :], st[:, i, :]), after=[t_s])
            t_v = dve.put(lambda e: e.tensor_scalar(inv[:, :], mo[:, :, 1], eps, None, ALU.add),
                          after=[t_s2])
            t_v = dve.put(lambda e: e.reciprocal(inv[:, :], inv[:, :]), after=[t_v])
            t_q = act.put(lambda e: e.activation(inv[:, :], inv[:, :], ACT.Sqrt), after=[t_v])
            return [dve.put(lambda e, i=i: e.tensor_scalar(
                xn_tile[:, i, :], x_tile[:, i, :], mo[:, i, 0:1], inv[:, i:i + 1],
                ALU.subtract, ALU.mult), after=[t_q] + after) for i in range(TT)]

        PARTS = 3 * HD
        ROWS = PARTS + 2
        SMAX, ST, PV_BANK, DEN_BANK = (0, 1, 2), (3, 4, 5), 6, 7
        early = Region(top=True)
        wproj_region = Region(top=True)
        k_stack, q_stack, v_group = [], [], []
        t_ones_rows, t_wproj, prob_sum_read = [], [], []
        a_k = [arrival(f"a_k{i}") for i in range(2)]
        a_q = [arrival(f"a_q{i}") for i in range(3)]
        a_m = [arrival(f"a_m{i}") for i in range(3)]
        a_vg = [arrival(f"a_vg{i}") for i in range(2)]
        XR = 4
        a_xr = [arrival(f"a_xr{i}") for i in range(XR)]
        a_x1 = [arrival(f"a_x1{i}") for i in range(2)]
        a_g = [arrival(f"a_g{i}") for i in range(2)]
        a_wp2 = arrival("a_wproj")
        N_MAX = GH * TT * NCH

        def set_ones_rows(i):
            t_ones_rows.append(pool.put(lambda e: e.memset(
                k_stack[i][PARTS:ROWS, :, :].bitcast(fp32), 1.0)))
            pool.hold([t_ones_rows[i]])

        units = [(b, g, h) for b in range(B) for g in range(NG) for h in range(NCH)]
        NU = len(units)
        PER_B = NG * NCH
        k_free, q_free, vg_free = [[], []], [[], [], []], [[], []]
        t_k, t_q, t_vg, t_m, t_g = {}, {}, {}, {}, {}

        def load_group(G):
            b, g = divmod(G, NG)
            at = D + g * P
            for n, part in enumerate((0, 1, 0)):
                t_k[G] = sp.move(
                    k_stack[G % 2][n * HD:(n + 1) * HD, :, :],
                    qk_dram[b, part, at:at + P, :].rearrange("(h d) t -> d h t", h=GH),
                    a_k[G % 2], after=k_free[G % 2])
            t_vg[G] = sp.move(
                v_group[G % 2][:, :, :],
                v_dram[b, :, g * P:(g + 1) * P].rearrange("(k p) f -> p k f", p=P),
                a_vg[G % 2], after=vg_free[G % 2])

        def load_q(u):
            b, g, h = units[u]
            for n, part in enumerate((0, 0, 1)):
                t_q[u] = sp.move(
                    q_stack[u % 3][n * HD:(n + 1) * HD, :, :],
                    qk_dram[b, part, g * P:(g + 1) * P, h * CH:(h + 1) * CH]
                    .rearrange("(h d) t -> d h t", h=GH),
                    a_q[u % 3], after=q_free[u % 3])

        gates_read = [[], []]

        def load_gates(b):
            for n, kind in enumerate((GATE1, GATE1_BIAS)):
                t_g[b] = sp.move(gates[b % 2][:, n, :], rows_dram[kind, b].partition_broadcast(P),
                                 a_g[b % 2], after=gates_read[b % 2])

        smax_banks = Ring(list(SMAX))
        st_banks = Ring(list(ST))

        def smax_tile(u, n):
            b, g, _ = units[u]
            G = b * NG + g
            h, rest = divmod(n, TT * NCH)
            i, kh = divmod(rest, NCH)
            i_b, bank, free = smax_banks.take()
            q, k = q_stack[u % 3], k_stack[G % 2]
            t_mm = pe.put(lambda e: e.matmul(
                psum[:, bank, :], q[0:PARTS, h, i * P:(i + 1) * P],
                k[0:PARTS, h, kh * CH:(kh + 1) * CH], start=True, stop=True),
                after=free + [t_k[G], t_q[u]])
            t_r = dve.put(lambda e: e.reduce_max(max_part[:, n:n + 1], psum[:, bank, :], AX.X),
                          after=[t_mm] + max_part_read)
            smax_banks.free[i_b] = [t_r]
            return t_r

        max_part_read, negmax_read = [], []

        def send_max(u, t_last):
            t_c = dve.put(lambda e: e.tensor_reduce(
                max_q[:, :], max_part[:, :].rearrange("p (n k) -> p n k", k=NCH), axis=AX.X,
                op=ALU.max), after=[t_last])
            max_part_read[:] = [t_c]
            i_b, bank, free = smax_banks.take()
            t_tr = pe.put(lambda e: e.transpose(psum[0:GH * TT, bank, 0:P], max_q[:, :],
                                                ident[:, :]), after=free + [t_c])
            t_hi = dve.put(lambda e: e.tensor_scalar(
                negmax_hi[:, :], psum[0:GH * TT, bank, 0:P], -1.0, None, ALU.mult),
                after=[t_tr] + negmax_read)
            t_lo = dve.put(lambda e: e.scalar_tensor_tensor(
                negmax_lo[:, :], psum[0:GH * TT, bank, 0:P], -1.0,
                negmax_hi[:, :].bitcast(fp32), ALU.mult, ALU.subtract), after=[t_hi])
            smax_banks.free[i_b] = [t_lo]
            for n, m in enumerate((negmax_hi, negmax_lo)):
                row = q_stack[u % 3][PARTS + n:PARTS + n + 1, :, :]
                t_m[u] = sp.move(row, m[:, :], a_m[u % 3],
                                 after=[t_hi, t_lo] + q_free[u % 3])
            negmax_read[:] = [t_m[u]]

        first_tokens = []

        def first_maximum():
            if len(first_tokens) < N_MAX:
                first_tokens.append(smax_tile(0, len(first_tokens)))

        x_read = [[], []]
        xn_read = []
        t_xn, t_h = {}, {}

        def load_x(c):
            if c < n_chunks:
                t_x[c] = sp.move(x_bufs[c % 2][:, :, :], x_chunk[c], a_x[c % 2],
                                 after=x_read[c % 2])

        def norm1(c):
            if c < n_chunks:
                t_xn[c] = normalise(x_bufs[c % 2], xn, stats, moments, inv_std, [t_x[c]], xn_read)
                x_read[c % 2] = t_xn[c]
                xn_read[:] = []

        def feature_block(c, f):
            if c >= n_chunks:
                return
            b = c // NCH
            i_h = c % 2
            hi, lo = hT.buffers[i_h]
            i_tr, bank, free = tr_banks.take()
            for i in range(TT):
                t_tr = pe.put(lambda e, i=i: e.transpose(
                    psum[:, bank, i * P:(i + 1) * P], xn[:, i, f * P:(f + 1) * P],
                    ident[:, :]), after=t_xn[c] + free, signal=(i == TT - 1))
            if f == KD - 1:
                xn_read[:] = [t_tr]
            i_f, full, f_free = h_full.take()
            t_f = dve.put(lambda e: e.tensor_scalar(
                full[:, :], psum[:, bank, :], ln_scale[:, 0, f, b:b + 1],
                ln_shift[:, 0, f, b:b + 1], ALU.mult, ALU.add),
                after=[t_tr] + t_ln1 + f_free)
            tr_banks.free[i_tr] = [t_f]
            t_hi = act.put(lambda e: e.activation(hi[:, f, :], full[:, :], ACT.Copy),
                           after=[t_f] + hT.free[i_h])
            t_lo = dve.put(lambda e: e.tensor_tensor(
                lo[:, f, :], full[:, :], hi[:, f, :].bitcast(fp32), ALU.subtract),
                after=[t_hi] + hT.free[i_h])
            h_full.free[i_f] = [t_lo]
            t_h.setdefault(c, []).extend([t_hi, t_lo])

        norm1(0)
        split_wqkv(0, wqkv_loads)
        wqkv_loads = load_wqkv(1)
        load_x(1)
        t_bv = sp.move(bv[:, :], t["bqkv"][2 * D:3 * D].partition_broadcast(P), a_bv)
        t_wt_gate = sp.move(wt[0][:, :, 2 * D:3 * D], wt_view[:, :, 2 * D:3 * D], a_wtg)
        t_wt[1] = [sp.move(wt[1][:, :, :], wt_view[:, :, 3 * D:6 * D], a_wt[1])]
        for f in range(KD):
            feature_block(0, f)
        split_wqkv(1, wqkv_loads)
        for c in range(n_chunks):
            b, half = divmod(c, NCH)
            i_h = c % 2
            hi, lo = hT.buffers[i_h]
            if c > 0:
                load_x(c + 1)
            last_chunk = c == n_chunks - 1
            if c == n_chunks - 2:
                while side_work:
                    next_side()
                for lane in (act, dve, pool, sp):
                    lane.hold(side_done)
                k_stack.append(early("k_stack0", [ROWS, GH, L], fp32r))
                q_stack += [early(f"q_stack{i}", [ROWS, GH, CH], fp32r) for i in range(2)]
                v_group.append(early("v_group0", [P, KT, P]))
                max_part = early("max_part", [P, N_MAX])
                max_q = early("max_q", [P, GH * TT])
                negmax_hi = early("negmax_hi", [GH * TT, P], fp32r)
                negmax_lo = early("negmax_lo", [GH * TT, P], fp32r)
                prob_sum = early("prob_sum", [P, GH, CH])
                wproj_hi = wproj_region("wproj_hi", [P, KD, D], fp32r)
                wproj_lo = wproj_region("wproj_lo", [P, KD, D], fp32r)
                set_ones_rows(0)
                load_group(0)
                load_q(0)
                load_q(1)
                t_raw = sp.move(prob_sum[:, :, :],
                                t["Wproj"].rearrange("(k p) n -> p k n", p=P), a_wp2)
            if last_chunk:
                smax_banks.free[0], smax_banks.free[1] = tr_banks.free
                smax_banks.free[2] = bank_free[SIDE_BANK]
                t_wproj += split_weights(prob_sum[:, :, :], wproj_hi[:, :, :],
                                         wproj_lo[:, :, :], [t_raw])
                prob_sum_read[:] = t_wproj
            for j in range(2 * KD):
                i_mm, bank, free = mm_banks.take()
                t_mm = three_pass(psum[:, bank, :], [
                    (wqkv_hi[:, k, j * P:(j + 1) * P], wqkv_lo[:, k, j * P:(j + 1) * P],
                     hi[:, k, :], lo[:, k, :]) for k in range(KD)],
                    after=free + t_h[c] + t_wqkv[(j + 1) * P > RAW],
                    between=first_maximum if last_chunk else None)
                i_o, o, o_free = qk_out.take()
                bias = cols[:, BQK + j:BQK + j + 1]
                t_a = act.put(lambda e, o=o, bank=bank, bias=bias: e.activation(
                    o[:, 0, :], psum[:, bank, :], ACT.Identity, bias=bias),
                    after=[t_mm, t_cols] + o_free)
                t_b = dve.put(lambda e, o=o, bank=bank, bias=bias: e.scalar_tensor_tensor(
                    o[:, 1, :], psum[:, bank, :], bias, o[:, 0, :].bitcast(fp32),
                    ALU.add, ALU.subtract), after=[t_a] + o_free)
                mm_banks.free[i_mm] = [t_b]
                t_st = sp.move(qk_dram[b, :, j * P:(j + 1) * P, half * CH:(half + 1) * CH]
                               .rearrange("s p t -> p s t"), o[:, :, :], a_qk[i_o],
                               after=[t_a, t_b])
                qk_out.free[i_o] = [t_st]
                if j == 1:
                    norm1(c + 1)
                if j >= KD:
                    feature_block(c + 1, j - KD)
                if j not in (1, 2):
                    next_side()
            if last_chunk:
                send_max(0, first_tokens[-1])
            for i in range(TT):
                i_mm, bank, free = mm_banks.take()
                t_mm = three_pass(psum[:, bank, :], [
                    (hi[:, k, i * P:(i + 1) * P], lo[:, k, i * P:(i + 1) * P],
                     wqkv_hi[:, k, 2 * D:3 * D], wqkv_lo[:, k, 2 * D:3 * D]) for k in range(KD)],
                    after=free)
                i_o, o, o_free = v_out.take()
                t_v = dve.put(lambda e, o=o, bank=bank: e.tensor_tensor(
                    o[:, :], psum[:, bank, :], bv[:, :], ALU.add), after=[t_mm, t_bv] + o_free)
                mm_banks.free[i_mm] = [t_v]
                at = half * CH + i * P
                t_st = sp.move(v_dram[b, at:at + P, :], o[:, :], a_v[i_o], after=[t_v])
                v_out.free[i_o] = [t_st]
            hT.free[i_h] = [t_mm]
        s1_done = everything()
        s1.close()

        for lane in (act, dve, pool, sp):
            lane.hold(s1_done)
        for i in range(len(ST)):
            st_banks.free[i] = mm_banks.free[i]
        s2 = sb = Region()
        k_stack.append(sb("k_stack1", [ROWS, GH, L], fp32r))
        set_ones_rows(1)
        q_stack.append(sb("q_stack2", [ROWS, GH, CH], fp32r))
        v_group.append(sb("v_group1", [P, KT, P]))
        probs = [sb(f"probs{i}", [P, GH, 2, CH]) for i in range(3)]
        project_region = Region(top=True)
        sb = project_region
        attn = [None, None]
        attn[(B - 1) % 2] = sb("attn_last", [P, NG, L])
        attn[B % 2] = s2("attn_other", [P, NG, L])
        attn_hi = [sb(f"attn_hi{i}", [P, NG, P], fp32r) for i in range(2)]
        attn_lo = [sb(f"attn_lo{i}", [P, NG, P], fp32r) for i in range(2)]
        x_res = [sb(f"x_res{i}", [P, D]) for i in range(XR)]
        x1_out = [sb(f"x1_out{i}", [P, D]) for i in range(2)]
        gates = [None, None]
        gates[(B - 1) % 2] = sb("gates_last", [P, 2, D])
        gates[B % 2] = s2("gates_other", [P, 2, D])
        den_inv = sb("den_inv", [P, CH])
        weighted = [sb(f"weighted{i}", [P, CH]) for i in range(2)]

        probs_read = [[], [], []]
        attn_hi_read = [[], []]
        attn_read = [[], []]
        attn_done = {}
        pv_free, den_free = list(mm_banks.free[3]), list(mm_banks.free[4])
        x1_read = [[], []]
        xr_read = [[] for _ in range(XR)]
        t_xr = {}

        def load_x_res(n):
            b, i = divmod(n, KT)
            t_xr[n] = sp.move(x_res[n % XR][:, :], t["x"][b, i * P:(i + 1) * P, :], a_xr[n % XR],
                              after=xr_read[n % XR])

        def project(n, ready=None):
            b, i = divmod(n, KT)
            src = attn[b % 2]
            cut = slice(i * P, (i + 1) * P)
            hi, lo = attn_hi[n % 2], attn_lo[n % 2]
            read = attn_hi_read[n % 2]
            t_hi = act.put(lambda e: e.activation(hi[:, :, :], src[:, :, cut], ACT.Copy),
                           after=(ready or attn_done[b]) + read)
            t_lo = dve.put(lambda e: e.tensor_tensor(
                lo[:, :, :], src[:, :, cut], hi[:, :, :].bitcast(fp32), ALU.subtract),
                after=[t_hi] + read)
            if i == KT - 1:
                attn_read[b % 2] = [t_hi, t_lo]
            t_xg = pool.put(lambda e: e.tensor_tensor(
                x_res[n % XR][:, :], x_res[n % XR][:, :], gates[b % 2][:, 1, :], ALU.add),
                after=[t_xr[n], t_g[b]])

            bank_of = []

            def first_half():
                i_b, bank, free = smax_banks.take()
                bank_of.extend((i_b, bank))
                products(range(KD // 2), free + [t_hi, t_lo] + t_wproj)

            def products(blocks, after):
                for k in blocks:
                    for a, w in ((hi, wproj_hi), (hi, wproj_lo), (lo, wproj_hi)):
                        last = k == KD - 1 and a is lo
                        t_mm = pe.put(lambda e, k=k, a=a, w=w, last=last: e.matmul(
                            psum[:, bank_of[1], :], a[:, k, :], w[:, k, :],
                            start=(k == 0 and a is hi and w is wproj_hi), stop=last),
                            after=after, signal=last)
                return t_mm

            def second_half():
                i_b, bank = bank_of
                t_mm = products(range(KD // 2, KD), ())
                attn_hi_read[n % 2] = [t_mm]
                o = x1_out[n % 2]
                t_y = dve.put(lambda e: e.tensor_tensor(
                    o[:, :], psum[:, bank, :], gates[b % 2][:, 0, :], ALU.mult),
                    after=[t_mm, t_g[b]] + x1_read[n % 2])
                smax_banks.free[i_b] = [t_y]
                t_x1 = dve.put(lambda e: e.tensor_tensor(
                    o[:, :], o[:, :], x_res[n % XR][:, :], ALU.add), after=[t_y, t_xg])
                xr_read[n % XR] = [t_x1]
                if i == KT - 1:
                    gates_read[b % 2] = [t_x1]
                x1_read[n % 2] = [sp.move(x1_dram[b, i * P:(i + 1) * P, :], o[:, :], a_x1[n % 2],
                                          after=[t_x1])]

            return first_half, second_half

        def slot(u, s):
            return (u * (KT // 2) + s) % len(probs)

        def value_products(u, s, j):
            b, g, _ = units[u]
            G = b * NG + g
            kt = 2 * s + j
            pb = probs[slot(u, s)]
            for h in range(GH):
                t_pv = pe.put(lambda e, h=h: e.matmul(
                    psum[h * HD:(h + 1) * HD, PV_BANK, :],
                    v_group[G % 2][:, kt, h * HD:(h + 1) * HD], pb[:, h, j, :],
                    start=(kt == 0), stop=(kt == KT - 1)),
                    after=(t_p[s] + [t_vg[G]] + pv_free) if h == 0 else (),
                    signal=(h == GH - 1))
            return t_pv

        load_gates(0)
        STEPS = KT // 2
        SUMMED = STEPS - 1
        LAST = KT // 2 - 1
        PROJ_LAG = PER_B + 1
        t_weighted, t_den = {}, {}
        weighted_read = [[], []]

        def sum_probs(u, s, t_p):
            pb = probs[slot(u, s)]
            if s == 0:
                t_sum = pool.put(lambda e: e.tensor_tensor(
                    prob_sum[:, :, :], pb[:, :, 0, :], pb[:, :, 1, :], ALU.add),
                    after=t_p + prob_sum_read)
            else:
                for j in range(2):
                    t_sum = pool.put(lambda e, j=j: e.tensor_tensor(
                        prob_sum[:, :, :], prob_sum[:, :, :], pb[:, :, j, :], ALU.add),
                        after=t_p + t_summed)
                    t_summed[:] = [t_sum]
            t_summed[:] = [t_sum]

        t_summed = []

        def denominators(u, n, last):
            term = prob_sum[:, :, :] if last else probs[slot(u, LAST)][:, :, n, :]
            for h in range(GH):
                t = pe.put(lambda e, h=h: e.matmul(
                    psum[h * HD:(h + 1) * HD, DEN_BANK, :], ones[:, :], term[:, h, :],
                    start=(n == 0), stop=last),
                    after=(t_summed if last else ()) or [t_ones] + den_free,
                    signal=(h == GH - 1))
            t_den[u] = t
            if last:
                prob_sum_read[:] = [t]
            else:
                probs_read[slot(u, LAST)] = probs_read[slot(u, LAST)] + [t]

        def normalise_attention(u):
            b, g, half = units[u]
            t_i = dve.put(lambda e: e.reciprocal(den_inv[:, :], psum[:, DEN_BANK, :]),
                          after=[t_den[u]])
            den_free[:] = [t_i]
            t_n = dve.put(lambda e: e.tensor_tensor(
                attn[b % 2][:, g, half * CH:(half + 1) * CH], weighted[u % 2][:, :],
                den_inv[:, :], ALU.mult), after=[t_i, t_weighted[u]] + attn_read[b % 2])
            weighted_read[u % 2] = [t_n]
            attn_done[b] = [t_n]

        for u, (b, g, half) in enumerate(units):
            G = b * NG + g
            if half == 0 and (G + 1) * NCH < NU:
                load_group(G + 1)
            if u + 2 < NU:
                load_q(u + 2)
            if u % PER_B == 1 and b >= 1:
                load_gates(b)
            tile = u - PROJ_LAG
            if tile >= 0:
                load_x_res(tile)
            t_p = {}
            max_tokens = []
            for s in range(KT // 2):
                pb = probs[slot(u, s)]
                t_p[s] = []
                if tile >= 0 and s == LAST:
                    first_half, second_half = project(tile)

                def scores(h, s=s, pb=pb):
                    q, k = q_stack[u % 3], k_stack[G % 2]
                    for j in range(2):
                        kt = 2 * s + j
                        i_b, bank, free = st_banks.take()
                        t_mm = pe.put(lambda e, bank=bank, kt=kt: e.matmul(
                            psum[:, bank, :], k[0:ROWS, h, kt * P:(kt + 1) * P],
                            q[0:ROWS, h, :], start=True, stop=True),
                            after=free + [t_m[u], t_q[u], t_k[G], t_ones_rows[G % 2]])
                        t_e = act.put(lambda e, bank=bank, j=j: e.activation(
                            pb[:, h, j, :], psum[:, bank, :], ACT.Exp, scale=SCALE),
                            after=[t_mm] + probs_read[slot(u, s)])
                        st_banks.free[i_b] = [t_e]
                    t_p[s].append(t_e)
                    return t_mm

                def maxima():
                    if u + 1 < NU:
                        max_tokens.append(smax_tile(u + 1, len(max_tokens)))

                for pair in range(GH // 2):
                    maxima()
                    t_mm = scores(2 * pair)
                    maxima()
                    if s > 0:
                        t_pv = value_products(u, s - 1, pair)
                    elif u > 0 and pair == 0:
                        denominators(u - 1, 0, False)
                        denominators(u - 1, 1, False)
                    elif u > 0:
                        denominators(u - 1, 2, True)
                    maxima()
                    t_mm = scores(2 * pair + 1)
                    maxima()
                if s > 0:
                    probs_read[slot(u, s - 1)] = [t_pv] + t_summed
                if s < SUMMED:
                    sum_probs(u, s, t_p[s])
                if s == 0 and u == NU - 1:
                    normalise_attention(u - 1)
            q_free[u % 3] = [t_mm]
            if half == NCH - 1:
                k_free[G % 2] = [t_mm]
            if tile >= 0:
                first_half()
            if u + 1 < NU:
                send_max(u + 1, max_tokens[-1])
            for j in range(2):
                t_pv = value_products(u, LAST, j)
            probs_read[slot(u, LAST)] = [t_pv]
            if half == NCH - 1:
                vg_free[G % 2] = [t_pv]
            t_weighted[u] = act.put(lambda e, u=u: e.activation(
                weighted[u % 2][:, :], psum[:, PV_BANK, :], ACT.Copy),
                after=[t_pv] + weighted_read[u % 2])
            pv_free[:] = [t_weighted[u]]
            if 0 < u < NU - 1:
                normalise_attention(u - 1)
            if tile >= 0:
                second_half()
        tail = list(range(NU - PROJ_LAG, B * KT))
        assert tail[0] >= TT, "stage 3 starts with a chunk that the tail would write"
        before_last = attn_done[B - 1]

        for tile in tail[:XR]:
            load_x_res(tile)
        first_half, second_half = project(tail[0])
        denominators(NU - 1, 0, False)
        denominators(NU - 1, 1, False)
        first_half()
        second_half()
        load_x_res(tail[XR])
        denominators(NU - 1, 2, True)
        s2_done = everything()
        halves = project(tail[1], before_last)
        normalise_attention(NU - 1)
        for region in (s2, early):
            region.close()
        for lane in (act, dve, pool, sp):
            lane.hold(s2_done)

        s3 = sb = Region()
        HB = 2
        NPC = KM // HB
        w1_hi, w1_lo, w2_hi, w2_lo = [], [], [], []
        w_raw_region = Region(top=True)
        w_raw = Ring([w_raw_region(f"w_raw{i}", [P, HB * D]) for i in range(3)])
        a_wr = [arrival(f"a_wr{i}") for i in range(3)]
        t_w1, t_w2 = [], []

        def piece_buffers(count):
            for _ in range(count):
                n = len(w1_hi)
                for part, name in ((w1_hi, "w1_hi"), (w1_lo, "w1_lo")):
                    part.append(s3(f"{name}{n}", [P, KD, HB * P], fp32r))
                for part, name in ((w2_hi, "w2_hi"), (w2_lo, "w2_lo")):
                    part.append(s3(f"{name}{n}", [P, HB, D], fp32r))

        def load_weights(m):
            n, which = divmod(m, 2)
            i_r, raw, free = w_raw.take()
            at = n * HB
            if which == 0:
                view = raw[:, :].rearrange("p (a b) -> p a b", a=KD)
                src = t["W1"].rearrange("(k p) m -> p k m", p=P)[:, :, at * P:(at + HB) * P]
                hi, lo, done = w1_hi, w1_lo, t_w1
            else:
                view = raw[:, :].rearrange("p (a b) -> p a b", a=HB)
                src = t["W2"].rearrange("(k p) m -> p k m", p=P)[:, at:at + HB, :]
                hi, lo, done = w2_hi, w2_lo, t_w2
            t_r = sp.move(view, src, a_wr[i_r], after=free)

            def split():
                t_s = split_weights(view, hi[n][:, :, :], lo[n][:, :, :], [t_r], pool)
                w_raw.free[i_r] = t_s
                done.append(t_s)

            return split

        pieces = iter(range(2 * NPC))
        loaded = []

        def next_weights():
            while len(loaded) < len(w_raw.buffers):
                m = next(pieces, None)
                if m is None:
                    break
                loaded.append(load_weights(m))
            loaded.pop(0)()

        piece_buffers(NPC // 2)
        loaded.append(load_weights(next(pieces)))
        x1 = [sb("x1_0", [P, TT, D])]
        xn_mlp = sb("xn2", [P, TT, D])
        h_hi = sb("h2_hi", [P, KD, CH], fp32r)
        h_lo = sb("h2_lo", [P, KD, CH], fp32r)
        work = Ring([sb(f"work{i}", [P, CH]) for i in range(4)])
        g_parts = Ring([sb(f"g_parts{i}", [P, 2, CH], fp32r) for i in range(3)])
        rows3 = sb("rows3", [P, 4, D])
        stats = sb("stats2", [P, TT, 6])
        moments = sb("moments2", [P, TT, 2])
        inv_std = sb("inv_std2", [P, TT])
        square_sum = sb("square_sum", [P, TT])
        a_x1r = [arrival(f"a_x1r{i}") for i in range(2)]
        a_r3 = arrival("a_rows3")
        a_y = [arrival(f"a_y{i}") for i in range(2)]
        ACC = (0, 1, 2, 3)
        tr_banks = Ring([4, 5])
        up_banks = Ring([6, 7])
        x1_free = [[], []]
        acc_free = [[] for _ in ACC]
        h_free, rows3_free, xn_read = [], [], []
        square_read = []
        t_x1, t_rows3, t_h = {}, {}, {}

        x1_written = []

        def load_x1(c):
            b, half = divmod(c, NCH)
            t_x1[c] = sp.move(x1[c % 2][:, :, :],
                              x1_dram[b, half * CH:(half + 1) * CH, :]
                              .rearrange("(t p) d -> p t d", p=P), a_x1r[c % 2],
                              after=x1_free[c % 2] + x1_written)

        def load_rows3(b):
            for n in range(4):
                t_rows3[b] = sp.move(rows3[:, n, :],
                                     rows_dram[GATE2 + n, b].partition_broadcast(P), a_r3,
                                     after=rows3_free)

        def add_bias(c):
            b = c // NCH
            return pool.put(lambda e: e.tensor_tensor(
                x1[c % 2][:, :, :], x1[c % 2][:, :, :],
                rows3[:, 1, :].unsqueeze(1).to_broadcast([P, TT, D]), ALU.add),
                after=[t_rows3[b]] + t_norm[c])

        t_norm, t_biased = {}, {}
        lag = []

        def up(c, i):
            piece, at = divmod(i, HB)
            cols_of_i = slice(at * P, (at + 1) * P)
            i_b, bank, free = up_banks.take()
            t_mm = three_pass(psum[:, bank, :], [
                (w1_hi[piece][:, k, cols_of_i], w1_lo[piece][:, k, cols_of_i],
                 h_hi[:, k, :], h_lo[:, k, :]) for k in range(KD)],
                after=free + t_h[c] + t_w1[piece])
            if i == KM - 1:
                h_free[:] = [t_mm]
            i_w, w, w_free = work.take()
            i_g, gp, g_free = g_parts.take()
            bias = cols[:, B1 + i:B1 + i + 1]
            t_f = act.put(lambda e: e.activation(w[:, :], psum[:, bank, :], ACT.Gelu, bias=bias),
                          after=[t_mm] + w_free)
            t_hi = act.put(lambda e: e.activation(gp[:, 0, :], psum[:, bank, :], ACT.Gelu,
                                                  bias=bias), after=g_free)
            up_banks.free[i_b] = [t_hi]
            t_lo = dve.put(lambda e: e.tensor_tensor(
                gp[:, 1, :], w[:, :], gp[:, 0, :].bitcast(fp32), ALU.subtract),
                after=[t_f, t_hi] + g_free)
            work.free[i_w] = [t_lo]

            def down():
                for n in range(TT):
                    cut = slice(n * P, (n + 1) * P)
                    pairs = ((0, w2_hi[piece]), (0, w2_lo[piece]), (1, w2_hi[piece]))
                    for m, (part, w2) in enumerate(pairs):
                        last = i == KM - 1 and m == 2
                        t_d = pe.put(lambda e, n=n, cut=cut, part=part, w2=w2, m=m, last=last:
                                     e.matmul(psum[:, ACC[n], :], gp[:, part, cut],
                                              w2[:, at, :], start=(i == 0 and m == 0),
                                              stop=last),
                                     after=([t_hi, t_lo] + t_w2[piece]
                                            + (acc_free[n] if i == 0 else [])) if m == 0 else (),
                                     signal=m == 2)
                    t_down[n] = t_d
                g_parts.free[i_g] = [t_d]

            return down

        t_down = [None] * TT

        def finish_first(c):
            b = c // NCH
            t_x2 = []
            for n in range(TT):
                i_w, w, w_free = work.take()
                t_y = dve.put(lambda e, n=n, w=w: e.tensor_tensor(
                    w[:, :], psum[:, ACC[n], :], rows3[:, 0, :], ALU.mult),
                    after=[t_down[n], t_rows3[b]] + w_free)
                acc_free[n] = [t_y]
                t_x2.append(dve.put(lambda e, n=n, w=w: e.tensor_tensor(
                    x1[c % 2][:, n, :], x1[c % 2][:, n, :], w[:, :], ALU.add),
                    after=[t_y, t_biased[c]]))
                work.free[i_w] = [t_x2[-1]]
            return t_x2

        def finish_second(c, t_x2):
            for n in range(TT):
                i_w, w, w_free = work.take()
                t_s = act.put(lambda e, n=n, w=w: e.activation(
                    w[:, :], x1[c % 2][:, n, :], ACT.Square,
                    accum_out=square_sum[:, n:n + 1]), after=[t_x2[n]] + w_free + square_read)
                work.free[i_w] = [t_s]
            t_r = dve.put(lambda e: e.tensor_scalar(
                square_sum[:, :], square_sum[:, :], 1.0 / D, RMS_EPS, ALU.mult, ALU.add),
                after=[t_s])
            t_r = dve.put(lambda e: e.reciprocal(square_sum[:, :], square_sum[:, :]),
                          after=[t_r])
            return act.put(lambda e: e.activation(square_sum[:, :], square_sum[:, :], ACT.Sqrt),
                           after=[t_r])

        def finish_third(c, t_r, n):
            b, half = divmod(c, NCH)
            i_y, y, y_free = y_out.take()
            t_a = dve.put(lambda e: e.scalar_tensor_tensor(
                y[:, :], x1[c % 2][:, n, :], square_sum[:, n:n + 1], rows3[:, 2, :],
                ALU.mult, ALU.mult), after=[t_r, t_rows3[b]] + y_free)
            t_b = pool.put(lambda e: e.tensor_tensor(y[:, :], y[:, :], rows3[:, 3, :], ALU.add),
                           after=[t_a])
            at = half * CH + n * P
            t_st = sp.move(out[b, at:at + P, :], y[:, :], a_y[i_y], after=[t_b])
            y_out.free[i_y] = [t_st]
            if n == TT - 1:
                square_read[:] = [t_a]
                x1_free[c % 2] = [t_a]
                rows3_free[:] = [t_b]

        def norm2(c):
            t_norm[c] = normalise(x1[c % 2], xn_mlp, stats, moments, inv_std, [t_x1[c]], xn_read)

        def transpose_h(c, blocks=range(KD)):
            b = c // NCH
            if blocks[0] == 0:
                t_h[c] = []
                xn_read[:] = []
            for f in blocks:
                i_tr, bank, free = tr_banks.take()
                for i in range(TT):
                    t_tr = pe.put(lambda e, i=i, f=f, bank=bank: e.transpose(
                        psum[:, bank, i * P:(i + 1) * P], xn_mlp[:, i, f * P:(f + 1) * P],
                        ident[:, :]), after=t_norm[c] + free, signal=(i == TT - 1))
                xn_read.append(t_tr)
                i_w, w, w_free = work.take()
                t_f = dve.put(lambda e, f=f, bank=bank, w=w: e.tensor_scalar(
                    w[:, :], psum[:, bank, :], ln_scale[:, 1, f, b:b + 1],
                    ln_shift[:, 1, f, b:b + 1], ALU.mult, ALU.add),
                    after=[t_tr] + t_ln2 + w_free)
                tr_banks.free[i_tr] = [t_f]
                t_hi = act.put(lambda e, f=f, w=w: e.activation(
                    h_hi[:, f, :], w[:, :], ACT.Copy), after=[t_f] + h_free)
                t_lo = dve.put(lambda e, f=f, w=w: e.tensor_tensor(
                    h_lo[:, f, :], w[:, :], h_hi[:, f, :].bitcast(fp32), ALU.subtract),
                    after=[t_hi] + h_free)
                work.free[i_w] = [t_lo]
                t_h[c] += [t_hi, t_lo]

        load_x1(0)
        loaded.append(load_weights(next(pieces)))
        tr_banks.free[:] = st_banks.free[1:3]
        up_banks.free[:] = [list(pv_free), list(den_free)]
        for n, tile in enumerate(tail[1:], 1):
            now = halves
            if n + 1 < len(tail):
                after_it = tail[n + 1]
                halves = project(after_it, before_last if after_it % KT < KT // 2 else None)
            for part in now:
                part()
            if n + XR < len(tail):
                load_x_res(tail[n + XR])
            if n == 3:
                norm2(0)
            if n in (5, 6):
                transpose_h(0, range(2 * n - 10, 2 * n - 8))
            if len(t_w2) < NPC // 2:
                next_weights()
        for m in range(TT - 1):
            acc_free[m] = smax_banks.free[m]
        acc_free[TT - 1] = st_banks.free[0]
        tail_done = everything()
        load_rows3(0)
        x1_written += tail_done
        for region in (wproj_region, project_region):
            region.close()
        while len(t_w2) < NPC // 2:
            next_weights()
        piece_buffers(NPC - NPC // 2)
        for c in range(n_chunks + 1):
            b, half = divmod(c, NCH)
            live = c < n_chunks
            if live and c > 0:
                transpose_h(c)
            for down in lag:
                down()
            lag = []
            if c >= 1:
                t_x2 = finish_first(c - 1)
            if live:
                for i in range(KM):
                    if c == 0 and i >= 2 and len(t_w2) < NPC:
                        if i == 2:
                            for lane in (act, dve, pool):
                                lane.hold(tail_done)
                        next_weights()
                        if len(t_w2) == NPC:
                            raw_free = [x for free in w_raw.free for x in free]
                            w_raw_region.close()
                            x1.append(s3("x1_1", [P, TT, D]))
                            y_out = Ring([s3(f"y_out{i}", [P, D]) for i in range(2)])
                            x1_free[1] = raw_free
                            y_out.free[:] = [raw_free, raw_free]
                    lag.append(up(c, i))
                    if len(lag) > 2:
                        lag.pop(0)()
                    if c >= 1 and i == 2:
                        t_r = finish_second(c - 1, t_x2)
                    if c >= 1 and 3 <= i < 3 + TT:
                        finish_third(c - 1, t_r, i - 3)
                    if i == 10 and c + 1 < n_chunks:
                        load_x1(c + 1)
                    if i == 9 and c > 0 and half == 0:
                        load_rows3(b)
                    if i == 10:
                        t_biased[c] = add_bias(c)
                    if i == 12 and c + 1 < n_chunks:
                        norm2(c + 1)
            else:
                t_r = finish_second(c - 1, t_x2)
                for n in range(TT):
                    finish_third(c - 1, t_r, n)
        s3.close()

        block = whole.enter_context(nc.Block())
        final = [(a.sem, a.value) for a in arrivals if a.value]
        for s_, v_ in final:
            sp.todo.append(lambda e, s_=s_, v_=v_: e.wait_ge(s_, v_))

        @block.sync
        def _(engine):
            sp.run(engine)

        @block.scalar
        def _(engine):
            act.run(engine)

        @block.vector
        def _(engine):
            dve.run(engine)

        @block.gpsimd
        def _(engine):
            pool.run(engine)

        @block.tensor
        def _(engine):
            pe.run(engine)


_SHORT = {"cond_1024": "cond"}


def kernel(**inputs):
    import concourse.bacc as bacc
    from concourse.bass_utils import run_bass_kernel_spmd

    nc = bacc.Bacc("TRN2", target_bir_lowering=False, num_devices=1)
    arrays, tensors = {}, {}
    for name, a in inputs.items():
        short = _SHORT.get(name, name.replace("L0_cond_", "").replace("L1_cond_", ""))
        a = np.ascontiguousarray(a)
        arrays[f"in_{short}"] = a
        tensors[short] = nc.dram_tensor(f"in_{short}", a.shape, mybir.dt.from_np(a.dtype),
                                        kind="ExternalInput").ap()
    x = arrays["in_x"]
    out = nc.dram_tensor("out_0", x.shape, mybir.dt.from_np(x.dtype), kind="ExternalOutput").ap()
    build_block(nc, tensors, out)
    result = run_bass_kernel_spmd(nc, [arrays], core_ids=[0])
    return result.results[0]["out_0"]
```

```python
import numpy as np
from contextlib import ExitStack

import concourse.bass as bass
from concourse import mybir


def build_block(nc, t, out):
    fp32 = mybir.dt.float32
    fp32r = mybir.dt.float32r
    ALU = mybir.AluOpType
    ACT = mybir.ActivationFunctionType
    AX = mybir.AxisListType

    class Lane:

        def __init__(self, done):
            self.done, self.count, self.todo, self.waited = done, 0, [], {}

        def put(self, make, after=(), signal=True):
            self.hold(after)
            if signal:
                self.count += 1
                self.todo.append(lambda e: make(e).then_inc(self.done, 1))
            else:
                self.todo.append(make)
            return (self.done, self.count)

        def hold(self, after):
            for sem, value in after:
                if self.waited.get(sem.name, 0) < value:
                    self.waited[sem.name] = value
                    self.todo.append(lambda e, s=sem, v=value: e.wait_ge(s, v))

        def move(self, dst, src, arrival, after=()):
            self.hold(after)
            arrival.value += 16
            dst, src = (v.bitcast(fp32) if v.dtype == fp32r else v for v in (dst, src))
            self.todo.append(lambda e: e.dma_start(dst, src).then_inc(arrival.sem, 16))
            return (arrival.sem, arrival.value)

        def run(self, engine):
            for make in self.todo:
                make(engine)

    class Arrival:

        def __init__(self, sem):
            self.sem, self.value = sem, 0

    class Ring:

        def __init__(self, buffers):
            self.buffers, self.free, self.turn = buffers, [[] for _ in buffers], 0

        def take(self):
            i = self.turn % len(self.buffers)
            self.turn += 1
            return i, self.buffers[i], self.free[i]

    B, L, D = t["x"].shape
    P = 128
    H, HD = 16, 32
    MLP = t["W1"].shape[1]
    KD = D // P
    KM = MLP // P
    CH = 512
    NCH = L // CH
    TT = CH // P
    NG = H * HD // P
    GH = P // HD
    KT = L // P
    LN_EPS, RMS_EPS, Q_EPS = 1e-5, 1e-6, 1e-5
    SCALE = float(HD) ** -0.5
    ROUND = 12582912.0

    whole = ExitStack()
    with whole:
        def sem(name):
            return whole.enter_context(nc.semaphore(name))

        ALIGN = 32
        holes = [[(nc.sbuf_base + ALIGN - 1) // ALIGN * ALIGN, nc.sbuf_top // ALIGN * ALIGN]]

        def place(name, shape, dt=fp32, top=False):
            size = -(-int(np.prod(shape[1:])) * 4 // ALIGN) * ALIGN
            fits = [x for x in holes if x[1] - x[0] >= size]
            assert fits, f"no room for {name}: {size} bytes, holes {holes}"
            if top:
                fits[-1][1] -= size
                at = fits[-1][1]
            else:
                at = fits[0][0]
                fits[0][0] += size
            return nc.alloc_sbuf_tensor_at(name, shape, dt, offset=at), (at, at + size)

        def give_back(ranges):
            cuts = sorted([list(x) for x in ranges] + [x for x in holes if x[0] < x[1]])
            holes[:] = []
            for lo, hi in cuts:
                if holes and holes[-1][1] == lo:
                    holes[-1][1] = hi
                else:
                    holes.append([lo, hi])

        class Region:

            def __init__(self, top=False):
                self.ranges, self.top = [], top

            def __call__(self, name, shape, dt=fp32):
                view, span = place(name, shape, dt, self.top)
                self.ranges.append(span)
                return view

            def close(self):
                give_back(self.ranges)
                self.ranges = []

        keep = Region()
        pe, act, dve, pool, sp = (Lane(sem(n)) for n in
                                  ("pe_done", "act_done", "dve_done", "pool_done", "sp_done"))
        lanes = (pe, act, dve, pool, sp)
        arrivals = []

        def arrival(name):
            arrivals.append(Arrival(sem(name)))
            return arrivals[-1]

        def everything():
            return ([(l.done, l.count) for l in lanes if l.count]
                    + [(a.sem, a.value) for a in arrivals if a.value])

        qk_dram = nc.dram_tensor("qk_parts", (B, 2, 2 * D, L), fp32, kind="Internal").ap()
        v_dram = nc.dram_tensor("v_rows", (B, L, D), fp32, kind="Internal").ap()
        x1_dram = nc.dram_tensor("x_after_attention", (B, L, D), fp32, kind="Internal").ap()
        rows_dram = nc.dram_tensor("cond_rows", (6, B, D), fp32, kind="Internal").ap()
        GATE1, GATE1_BIAS, GATE2, GATE2_BIAS, RMS_SCALE, RMS_SHIFT = range(6)

        psum = whole.enter_context(nc.psum_tensor("psum", [P, 8, 512], fp32))
        bank_free = [[] for _ in range(8)]

        ident = keep("ident", [P, P])
        ones = keep("ones", [P, HD])
        cols = keep("cols", [P, 64])
        ln_scale = keep("ln_scale", [P, 2, KD, B])
        ln_shift = keep("ln_shift", [P, 2, KD, B])
        t_z = pool.put(lambda e: e.memset(ident[:, :], 0.0))
        t_ident = pool.put(lambda e: e.affine_select(
            out=ident[:, :], in_=ident[:, :], compare_op=ALU.not_equal, fill=1.0, base=0,
            pattern=[[-1, P]], channel_multiplier=1), after=[t_z])
        t_ones = pool.put(lambda e: e.memset(ones[:, :], 1.0))

        def three_pass(dst, terms, after, between=None):
            parts = []
            for lh, ll, rh, rl in terms:
                parts += [(lh, rh), (lh, rl), (ll, rh)]
            token = None
            for n, (a, b) in enumerate(parts):
                last = n == len(parts) - 1
                if between and n % 3 == 0:
                    between()
                token = pe.put(lambda e, a=a, b=b, n=n, last=last: e.matmul(
                    dst, a, b, start=(n == 0), stop=last),
                    after=after if n == 0 else (), signal=last)
            return token

        def split_weights(raw, hi, lo, after, subtract=None):
            t_hi = act.put(lambda e: e.activation(hi, raw, ACT.Copy), after=after)
            t_lo = (subtract or dve).put(
                lambda e: e.tensor_tensor(lo, raw, hi.bitcast(fp32), ALU.subtract),
                after=list(after) + [t_hi])
            return [t_hi, t_lo]

        s1 = sb = Region()
        wqkv_hi = sb("wqkv_hi", [P, KD, 3 * D], fp32r)
        wqkv_lo = sb("wqkv_lo", [P, KD, 3 * D], fp32r)
        x_bufs = [sb(f"x_in{i}", [P, TT, D]) for i in range(2)]
        xn = sb("xn", [P, TT, D])
        h_full = Ring([sb(f"h_full{i}", [P, CH]) for i in range(2)])
        hT = Ring([(sb(f"hT_hi{i}", [P, KD, CH], fp32r), sb(f"hT_lo{i}", [P, KD, CH], fp32r))
                   for i in range(2)])
        qk_out = Ring([sb(f"qk_out{i}", [P, 2, CH], fp32r) for i in range(3)])
        v_out = Ring([sb(f"v_out{i}", [P, D]) for i in range(3)])
        bv = sb("bv", [P, D])
        stats = sb("stats", [P, TT, 6])
        moments = sb("moments", [P, TT, 2])
        inv_std = sb("inv_std", [P, TT])
        a_x = [arrival(f"a_x{i}") for i in range(2)]
        a_qk = [arrival(f"a_qk{i}") for i in range(3)]
        a_v = [arrival(f"a_v{i}") for i in range(3)]
        a_bv = arrival("a_bv")
        n_chunks = B * NCH
        SIDE_BANK = 2
        mm_banks = Ring([3, 4, 5, 6, 7])
        tr_banks = Ring([0, 1])

        s0 = sb0 = Region()
        wt = [sb0(f"wt{i}", [P, KD, 3 * D]) for i in range(2)]
        RAW = 3 * D // 2
        wqkv_raw = Ring([sb0(f"wqkv_raw{i}", [P, RAW]) for i in range(KD)])
        cond = sb0("cond", [B, D])
        silu = sb0("silu", [B, D])
        siluT = sb0("siluT", [P, KD, B])
        vec_rows = sb0("vec_rows", [64, P])
        row_bias = sb0("row_bias", [B, 2, D])
        rows = sb0("rows", [B, 2, D])
        ln_tmp = [sb0(f"ln_tmp{i}", [P, KD, B]) for i in range(2)]
        a_cond, a_vec, a_rowb = arrival("a_cond"), arrival("a_vec"), arrival("a_row_bias")
        a_wt = [arrival(f"a_wt{i}") for i in range(2)]
        a_wtg = arrival("a_wt_gate")
        a_wraw = [arrival(f"a_wraw{i}") for i in range(KD)]
        a_rows = arrival("a_rows")

        wt_view = t["Wt"].rearrange("(k p) n -> p k n", p=P)
        x_chunk = [t["x"][b, c * CH:(c + 1) * CH, :].rearrange("(t p) d -> p t d", p=P)
                   for b in range(B) for c in range(NCH)]
        t_x = [None] * len(x_chunk)
        t_cond = sp.move(cond[:, :], t["cond"], a_cond)
        t_x[0] = sp.move(x_bufs[0][:, :, :], x_chunk[0], a_x[0])
        for name, at, n in (("bt", 0, 24), ("g1", 24, 4), ("be1", 28, 4), ("g2", 32, 4),
                            ("be2", 36, 4), ("bqkv", 40, 8), ("b1", 48, KM)):
            t_vec = sp.move(vec_rows[at:at + n, :],
                            t[name][0:n * P].rearrange("(n p) -> n p", p=P), a_vec)
        BT, GAMMA, BETA, BQK, B1 = 0, (24, 32), (28, 36), 40, 48
        t_wt = [[sp.move(wt[0][:, :, 0:2 * D], wt_view[:, :, 0:2 * D], a_wt[0])], None]
        t_wqkv = [[], []]

        def load_wqkv(n):
            loads = []
            for k in range(KD):
                i_r, raw, free = wqkv_raw.take()
                loads.append(sp.move(raw[:, :], t["Wqkv"][k * P:(k + 1) * P,
                                                          n * RAW:(n + 1) * RAW],
                                     a_wraw[i_r], after=free))
            return loads

        def split_wqkv(n, loads):
            cut = slice(n * RAW, (n + 1) * RAW)
            for k in range(KD):
                t_s = split_weights(wqkv_raw.buffers[k][:, :], wqkv_hi[:, k, cut],
                                    wqkv_lo[:, k, cut], [loads[k]], pool)
                wqkv_raw.free[k] = t_s
                t_wqkv[n] += t_s

        wqkv_loads = load_wqkv(0)

        t_silu = act.put(lambda e: e.activation(silu[:, :], cond[:, :], ACT.Silu), after=[t_cond])
        for k in range(KD):
            t_tr = pe.put(lambda e, k=k: e.transpose(
                psum[:, mm_banks.buffers[0], k * B:(k + 1) * B], silu[:, k * P:(k + 1) * P],
                ident[0:B, 0:B]), after=[t_silu, t_ident])
        t_siluT = dve.put(lambda e: e.tensor_copy(
            siluT[:, :, :], psum[:, mm_banks.buffers[0], 0:KD * B]
            .rearrange("p (k b) -> p k b", k=KD)), after=[t_tr])
        mm_banks.free[0] = [t_siluT]
        t_tr = pe.put(lambda e: e.transpose(psum[:, mm_banks.buffers[1], 0:64], vec_rows[:, :],
                                            ident[0:64, 0:64]), after=[t_vec])
        t_cols = dve.put(lambda e: e.tensor_copy(cols[:, :], psum[:, mm_banks.buffers[1], 0:64]),
                         after=[t_tr])
        mm_banks.free[1] = [t_cols]

        def norm_vectors(half):
            bank = SIDE_BANK
            for j in range(2 * KD):
                for k in range(KD):
                    t_mm = pe.put(lambda e, k=k, j=j: e.matmul(
                        psum[:, bank, j * B:(j + 1) * B], wt[half][:, k, j * P:(j + 1) * P],
                        siluT[:, k, :], start=(k == 0), stop=(k == KD - 1)),
                        after=[t_siluT] + t_wt[half] + bank_free[bank], signal=(k == KD - 1))
            shift, scale = ln_shift[:, half, :, :], ln_scale[:, half, :, :]
            view = psum[:, bank, 0:2 * KD * B].rearrange("p (s k b) -> p s k b", s=2, k=KD)

            def col(at):
                return cols[:, at:at + KD].unsqueeze(2).to_broadcast([P, KD, B])

            bt_at = BT + half * 3 * KD
            t_a = dve.put(lambda e: e.tensor_tensor(shift, view[:, 0, :, :], col(bt_at), ALU.add),
                          after=[t_mm, t_cols])
            t_b = dve.put(lambda e: e.scalar_tensor_tensor(
                scale, view[:, 1, :, :], 1.0, col(bt_at + KD), ALU.add, ALU.add),
                after=[t_mm, t_cols])
            bank_free[bank] = [t_b]
            tmp = ln_tmp[half]
            t_c = dve.put(lambda e: e.tensor_tensor(tmp[:, :, :], scale, col(BETA[half]), ALU.mult),
                          after=[t_b])
            t_shift = dve.put(lambda e: e.tensor_tensor(shift, shift, tmp[:, :, :], ALU.add),
                              after=[t_a, t_c])
            t_scale = dve.put(lambda e: e.tensor_tensor(scale, scale, col(GAMMA[half]), ALU.mult),
                              after=[t_c])
            return [t_shift, t_scale]

        t_ln1, t_ln2 = [], []
        s0_done, side_done = [], []

        def condition():
            yield
            t_ln2.extend(norm_vectors(1))
            yield
            t_rows = []
            for half, (bt_at, bias) in enumerate(((2 * D, "bproj"), (5 * D, "b2"))):
                bank = SIDE_BANK
                for n, src in enumerate((t["bt"][bt_at:bt_at + D], t[bias][0:D])):
                    t_rowb = sp.move(row_bias[:, n, :], src.partition_broadcast(B), a_rowb,
                                     after=t_rows)
                for k in range(KD):
                    t_mm = pe.put(lambda e, k=k, half=half: e.matmul(
                        psum[0:B, bank, :], siluT[:, k, :], wt[half][:, k, 2 * D:3 * D],
                        start=(k == 0), stop=(k == KD - 1)),
                        after=[t_siluT, t_wt_gate] + t_wt[1] + bank_free[bank],
                        signal=(k == KD - 1))
                t_g = dve.put(lambda e: e.tensor_tensor(
                    rows[:, 0, :], psum[0:B, bank, :], row_bias[:, 0, :], ALU.add),
                    after=[t_mm, t_rowb] + t_rows)
                bank_free[bank] = [t_g]
                t_gb = dve.put(lambda e: e.tensor_tensor(
                    rows[:, 1, :], rows[:, 0, :], row_bias[:, 1, :], ALU.mult), after=[t_g])
                t_rows = [sp.move(
                    rows_dram[2 * half:2 * half + 2, :, :].rearrange("n b d -> b n d"),
                    rows[:, :, :], a_rows, after=[t_g, t_gb])]
                yield
            s0_done.extend(everything())
            yield

        side_work = [condition()]

        def next_side():
            while side_work and next(side_work[0], "end") == "end":
                side_work.pop(0)

        WR = t["w_proj"].shape[0] // P
        sq = sbq = Region()
        a_wp, a_cq, a_ob = arrival("a_wp"), arrival("a_cq"), arrival("a_out_bias")

        def quantise():
            s0.close()
            wp = sbq("wp", [P, WR, D])
            wq_tmp = [sbq(f"wq_tmp{i}", [P, D]) for i in range(2)]
            wpT = sbq("wpT", [P, KD, WR * P])
            cq = sbq("cq", [B, D])
            cq_tmp = sbq("cq_tmp", [B, D])
            cqT = sbq("cqT", [P, KD, B])
            small = sbq("small", [P, 16])
            ones_sq = sbq("ones_sq", [P, P])
            out_bias = sbq("out_bias", [B, 3, D])
            emb = sbq("emb", [B, 2, D])
            t_emb = []
            t_wp = sp.move(wp[:, :, :], t["w_proj"].rearrange("(r p) c -> p r c", p=P), a_wp,
                           after=s0_done)
            t_cq = sp.move(cq[:, :], t["cond"], a_cq, after=s0_done)
            for n, src in enumerate((t["b_proj"][0:D], t["b_proj"][D:2 * D], t["rms_weight"])):
                t_ob = sp.move(out_bias[:, n, :], src.partition_broadcast(B), a_ob)
            t_o = pool.put(lambda e: e.memset(ones_sq[:, :], 1.0), after=s0_done)
            for r in range(WR):
                t_abs = dve.put(lambda e, r=r: e.tensor_reduce(
                    small[:, 8 + r:9 + r], wp[:, r, :], axis=AX.X, op=ALU.add,
                    apply_absolute_value=True), after=[t_wp] + s0_done)
                if r % 2:
                    yield
            t_abs = dve.put(lambda e: e.reduce_sum(small[:, 0:1], small[:, 8:8 + WR], AX.X),
                            after=[t_abs])
            yield
            yield
            bank = SIDE_BANK
            t_sum = pe.put(lambda e: e.matmul(psum[:, bank, 0:1], ones_sq[:, :], small[:, 0:1],
                                              start=True, stop=True),
                           after=[t_o, t_abs] + bank_free[bank])
            t_1 = dve.put(lambda e: e.tensor_scalar(
                small[:, 1:2], psum[:, bank, 0:1], 1.0 / (WR * P * D), Q_EPS, ALU.mult, ALU.max),
                after=[t_sum])
            t_2 = dve.put(lambda e: e.reciprocal(small[:, 2:3], small[:, 1:2]), after=[t_1])
            t_3 = dve.put(lambda e: e.reciprocal(small[:, 3:4], small[:, 2:3]), after=[t_2])
            bank_free[bank] = [t_1]
            yield
            tr_read = [[], []]
            for r in range(WR):
                tmp = wq_tmp[r % 2]
                row = wp[:, r, :]
                t_a = dve.put(lambda e, o=tmp, i=row: e.tensor_scalar(
                    o[:, :], i, small[:, 2:3], ROUND, ALU.mult, ALU.add), after=[t_2])
                t_a = dve.put(lambda e, o=tmp: e.tensor_scalar(
                    o[:, :], o[:, :], ROUND, -1.0, ALU.subtract, ALU.max), after=[t_a])
                t_a = dve.put(lambda e, o=tmp: e.tensor_scalar(
                    o[:, :], o[:, :], 1.0, small[:, 3:4], ALU.min, ALU.mult), after=[t_a, t_3])
                t_a = dve.put(lambda e, o=tmp, i=row: e.tensor_tensor(
                    o[:, :], o[:, :], i, ALU.subtract), after=[t_a])
                t_w = dve.put(lambda e, o=tmp, i=row: e.tensor_tensor(i, i, o[:, :], ALU.add),
                              after=[t_a])
                yield
                yield
                yield
                for k in range(KD):
                    t_tr = pe.put(lambda e, r=r, k=k: e.transpose(
                        psum[:, bank, k * P:(k + 1) * P], wp[:, r, k * P:(k + 1) * P],
                        ident[:, :]), after=[t_w] + bank_free[bank])
                t_wT = act.put(lambda e, r=r: e.activation(
                    wpT[:, :, r * P:(r + 1) * P],
                    psum[:, bank, :].rearrange("p (k d) -> p k d", k=KD), ACT.Copy),
                    after=[t_tr] + s0_done)
                bank_free[bank] = [t_wT]
            t_m = dve.put(lambda e: e.tensor_reduce(
                small[0:B, 4:5], cq[:, :], axis=AX.X, op=ALU.max, apply_absolute_value=True),
                after=[t_cq])
            t_m = dve.put(lambda e: e.tensor_scalar(
                small[0:B, 5:6], small[0:B, 4:5], Q_EPS, None, ALU.max), after=[t_m])
            t_m = dve.put(lambda e: e.reciprocal(small[0:B, 6:7], small[0:B, 5:6]), after=[t_m])
            t_m = dve.put(lambda e: e.tensor_scalar(
                small[0:B, 7:8], small[0:B, 6:7], 127.0, None, ALU.mult), after=[t_m])
            t_i = dve.put(lambda e: e.reciprocal(small[0:B, 8:9], small[0:B, 7:8]), after=[t_m])
            t_a = dve.put(lambda e: e.tensor_scalar(
                cq_tmp[:, :], cq[:, :], small[0:B, 7:8], ROUND, ALU.mult, ALU.add), after=[t_m])
            t_a = dve.put(lambda e: e.tensor_scalar(
                cq_tmp[:, :], cq_tmp[:, :], ROUND, -128.0, ALU.subtract, ALU.max), after=[t_a])
            t_a = dve.put(lambda e: e.tensor_scalar(
                cq_tmp[:, :], cq_tmp[:, :], 127.0, small[0:B, 8:9], ALU.min, ALU.mult),
                after=[t_a, t_i])
            t_a = dve.put(lambda e: e.tensor_tensor(
                cq_tmp[:, :], cq_tmp[:, :], cq[:, :], ALU.subtract), after=[t_a])
            t_a = dve.put(lambda e: e.tensor_tensor(
                cq[:, :], cq[:, :], cq_tmp[:, :], ALU.add), after=[t_a])
            yield
            yield
            yield
            for k in range(KD):
                t_tr = pe.put(lambda e, k=k: e.transpose(
                    psum[:, bank, k * B:(k + 1) * B], cq[:, k * P:(k + 1) * P],
                    ident[0:B, 0:B]), after=[t_a] + bank_free[bank])
            t_cqT = dve.put(lambda e: e.tensor_copy(
                cqT[:, :, :], psum[:, bank, 0:KD * B].rearrange("p (k b) -> p k b", k=KD)),
                after=[t_tr])
            bank_free[bank] = [t_cqT]
            yield
            for n in range(2):
                for k in range(KD):
                    t_mm = pe.put(lambda e, n=n, k=k: e.matmul(
                        psum[0:B, bank, :], cqT[:, k, :], wpT[:, k, n * D:(n + 1) * D],
                        start=(k == 0), stop=(k == KD - 1)),
                        after=[t_cqT, t_wT] + bank_free[bank], signal=(k == KD - 1))
                t_e = dve.put(lambda e, n=n: e.tensor_tensor(
                    emb[:, n, :], psum[0:B, bank, :], out_bias[:, n, :], ALU.add),
                    after=[t_mm, t_ob])
                bank_free[bank] = [t_e]
                t_emb.append(t_e)
            t_e = dve.put(lambda e: e.scalar_tensor_tensor(
                emb[:, 0, :], emb[:, 0, :], 1.0, out_bias[:, 2, :], ALU.add, ALU.mult),
                after=[t_emb[0]])
            sp.move(rows_dram[4:6, :, :].rearrange("n b d -> b n d"), emb[:, :, :], a_rows,
                    after=[t_e, t_emb[1]])
            side_done.extend(everything())
            sq.close()
            yield

        side_work.append(quantise())

        def normalise(x_tile, xn_tile, st, mo, inv, t_in, after, eps=LN_EPS):
            for i in range(TT):
                t_s = dve.put(lambda e, i=i: e.bn_stats(st[:, i, :], x_tile[:, i, :]),
                              after=t_in + after)
            for i in range(TT):
                t_s2 = dve.put(lambda e, i=i: e.bn_aggr(mo[:, i, :], st[:, i, :]), after=[t_s])
            t_v = dve.put(lambda e: e.tensor_scalar(inv[:, :], mo[:, :, 1], eps, None, ALU.add),
                          after=[t_s2])
            t_v = dve.put(lambda e: e.reciprocal(inv[:, :], inv[:, :]), after=[t_v])
            t_q = act.put(lambda e: e.activation(inv[:, :], inv[:, :], ACT.Sqrt), after=[t_v])
            return [dve.put(lambda e, i=i: e.tensor_scalar(
                xn_tile[:, i, :], x_tile[:, i, :], mo[:, i, 0:1], inv[:, i:i + 1],
                ALU.subtract, ALU.mult), after=[t_q] + after) for i in range(TT)]

        PARTS = 3 * HD
        ROWS = PARTS + 2
        SMAX, ST, PV_BANK, DEN_BANK = (0, 1, 2), (3, 4, 5), 6, 7
        early = Region(top=True)
        wproj_region = Region(top=True)
        k_stack, q_stack, v_group = [], [], []
        t_ones_rows, t_wproj, prob_sum_read = [], [], []
        a_k = [arrival(f"a_k{i}") for i in range(2)]
        a_q = [arrival(f"a_q{i}") for i in range(3)]
        a_m = [arrival(f"a_m{i}") for i in range(3)]
        a_vg = [arrival(f"a_vg{i}") for i in range(2)]
        XR = 4
        a_xr = [arrival(f"a_xr{i}") for i in range(XR)]
        a_x1 = [arrival(f"a_x1{i}") for i in range(2)]
        a_g = [arrival(f"a_g{i}") for i in range(2)]
        a_wp2 = arrival("a_wproj")
        N_MAX = GH * TT * NCH
        STEPS = KT // 2
        ORDER = (("mssm*mssm", "mssmm*mssmm"), ("mssm*mssm", "mssm*ssm"),
                 ("mssm*ssm", "mssm*ssm"), ("mssm*!mssm", "mssmm*mssm"))
        assert sum(x.count("m") for step in ORDER for x in step) == N_MAX
        LEAD = sum(x.count("m") for x in ORDER[-1])

        def set_ones_rows(i):
            t_ones_rows.append(pool.put(lambda e: e.memset(
                k_stack[i][PARTS:ROWS, :, :].bitcast(fp32), 1.0)))
            pool.hold([t_ones_rows[i]])

        units = [(b, g, h) for b in range(B) for g in range(NG) for h in range(NCH)]
        NU = len(units)
        PER_B = NG * NCH
        k_free, q_free, vg_free = [[], []], [[], [], []], [[], []]
        t_k, t_q, t_vg, t_m, t_g = {}, {}, {}, {}, {}

        def load_keys(G):
            b, g = divmod(G, NG)
            at = D + g * P
            for n, part in enumerate((0, 1, 0)):
                t_k[G] = sp.move(
                    k_stack[G % 2][n * HD:(n + 1) * HD, :, :],
                    qk_dram[b, part, at:at + P, :].rearrange("(h d) t -> d h t", h=GH),
                    a_k[G % 2], after=k_free[G % 2])

        def load_values(G):
            b, g = divmod(G, NG)
            t_vg[G] = sp.move(
                v_group[G % 2][:, :, :],
                v_dram[b, :, g * P:(g + 1) * P].rearrange("(k p) f -> p k f", p=P),
                a_vg[G % 2], after=vg_free[G % 2])

        def load_q(u):
            b, g, h = units[u]
            for n, part in enumerate((0, 0, 1)):
                t_q[u] = sp.move(
                    q_stack[u % 3][n * HD:(n + 1) * HD, :, :],
                    qk_dram[b, part, g * P:(g + 1) * P, h * CH:(h + 1) * CH]
                    .rearrange("(h d) t -> d h t", h=GH),
                    a_q[u % 3], after=q_free[u % 3])

        gates_read = [[], []]

        def load_gates(b):
            for n, kind in enumerate((GATE1, GATE1_BIAS)):
                t_g[b] = sp.move(gates[b % 2][:, n, :], rows_dram[kind, b].partition_broadcast(P),
                                 a_g[b % 2], after=gates_read[b % 2])

        smax_banks = Ring(list(SMAX))
        st_banks = Ring(list(ST))

        def smax_tile(u, n):
            b, g, _ = units[u]
            G = b * NG + g
            h, rest = divmod(n, TT * NCH)
            i, kh = divmod(rest, NCH)
            i_b, bank, free = smax_banks.take()
            q, k = q_stack[u % 3], k_stack[G % 2]
            t_mm = pe.put(lambda e: e.matmul(
                psum[:, bank, :], q[0:PARTS, h, i * P:(i + 1) * P],
                k[0:PARTS, h, kh * CH:(kh + 1) * CH], start=True, stop=True),
                after=free + [t_k[G], t_q[u]])
            t_r = dve.put(lambda e: e.reduce_max(max_part[:, n:n + 1], psum[:, bank, :], AX.X),
                          after=[t_mm] + max_part_read)
            smax_banks.free[i_b] = [t_r]
            return t_r

        max_part_read, max_q_read, negmax_read, to_send = [], [], [], []

        def gather_max(u, t_last):
            t_c = dve.put(lambda e: e.tensor_reduce(
                max_q[:, :], max_part[:, :].rearrange("p (n k) -> p n k", k=NCH), axis=AX.X,
                op=ALU.max), after=[t_last] + max_q_read)
            max_part_read[:] = [t_c]
            to_send.append((u, t_c))

        def send_max():
            u, t_c = to_send.pop()
            i_b, bank, free = smax_banks.take()
            t_tr = pe.put(lambda e: e.transpose(psum[0:GH * TT, bank, 0:P], max_q[:, :],
                                                ident[:, :]), after=free + [t_c])
            max_q_read[:] = [t_tr]
            t_hi = dve.put(lambda e: e.tensor_scalar(
                negmax_hi[:, :], psum[0:GH * TT, bank, 0:P], -1.0, None, ALU.mult),
                after=[t_tr] + negmax_read)
            t_lo = dve.put(lambda e: e.scalar_tensor_tensor(
                negmax_lo[:, :], psum[0:GH * TT, bank, 0:P], -1.0,
                negmax_hi[:, :].bitcast(fp32), ALU.mult, ALU.subtract), after=[t_hi])
            smax_banks.free[i_b] = [t_lo]
            for n, m in enumerate((negmax_hi, negmax_lo)):
                row = q_stack[u % 3][PARTS + n:PARTS + n + 1, :, :]
                t_m[u] = sp.move(row, m[:, :], a_m[u % 3],
                                 after=[t_hi, t_lo] + q_free[u % 3])
            negmax_read[:] = [t_m[u]]

        maxima_done = []

        def next_maximum():
            u, n = divmod(len(maxima_done), N_MAX)
            if u < NU:
                maxima_done.append(smax_tile(u, n))
                if n == N_MAX - 1:
                    gather_max(u, maxima_done[-1])

        def early_maximum():
            if len(maxima_done) < N_MAX + LEAD:
                next_maximum()

        x_read = [[], []]
        xn_read = []
        t_xn, t_h = {}, {}

        def load_x(c):
            if c < n_chunks:
                t_x[c] = sp.move(x_bufs[c % 2][:, :, :], x_chunk[c], a_x[c % 2],
                                 after=x_read[c % 2])

        def norm1(c):
            if c < n_chunks:
                t_xn[c] = normalise(x_bufs[c % 2], xn, stats, moments, inv_std, [t_x[c]], xn_read)
                x_read[c % 2] = t_xn[c]
                xn_read[:] = []

        def feature_block(c, f):
            b = c // NCH
            i_h = c % 2
            hi, lo = hT.buffers[i_h]
            i_tr, bank, free = tr_banks.take()
            for i in range(TT):
                t_tr = pe.put(lambda e, i=i: e.transpose(
                    psum[:, bank, i * P:(i + 1) * P], xn[:, i, f * P:(f + 1) * P],
                    ident[:, :]), after=t_xn[c] + free, signal=(i == TT - 1))
            if f == KD - 1:
                xn_read[:] = [t_tr]
            i_f, full, f_free = h_full.take()
            t_f = dve.put(lambda e: e.tensor_scalar(
                full[:, :], psum[:, bank, :], ln_scale[:, 0, f, b:b + 1],
                ln_shift[:, 0, f, b:b + 1], ALU.mult, ALU.add),
                after=[t_tr] + t_ln1 + f_free)
            tr_banks.free[i_tr] = [t_f]
            t_hi = act.put(lambda e: e.activation(hi[:, f, :], full[:, :], ACT.Copy),
                           after=[t_f] + hT.free[i_h])

            def subtract():
                t_lo = dve.put(lambda e: e.tensor_tensor(
                    lo[:, f, :], full[:, :], hi[:, f, :].bitcast(fp32), ALU.subtract),
                    after=[t_hi] + hT.free[i_h])
                h_full.free[i_f] = [t_lo]
                t_h.setdefault(c, []).extend([t_hi, t_lo])

            return subtract

        norm1(0)
        t_ln1 += norm_vectors(0)
        split_wqkv(0, wqkv_loads)
        wqkv_loads = load_wqkv(1)
        load_x(1)
        t_bv = sp.move(bv[:, :], t["bqkv"][2 * D:3 * D].partition_broadcast(P), a_bv)
        t_wt_gate = sp.move(wt[0][:, :, 2 * D:3 * D], wt_view[:, :, 2 * D:3 * D], a_wtg)
        t_wt[1] = [sp.move(wt[1][:, :, :], wt_view[:, :, 3 * D:6 * D], a_wt[1])]
        early_loads = []
        subtractions = []
        for f in range(KD):
            subtractions.append(feature_block(0, f))
            if f > 0:
                subtractions.pop(0)()
        subtractions.pop()()
        split_wqkv(1, wqkv_loads)
        for c in range(n_chunks):
            b, half = divmod(c, NCH)
            i_h = c % 2
            hi, lo = hT.buffers[i_h]
            if c > 0:
                load_x(c + 1)
            last_chunk = c == n_chunks - 1
            if c == n_chunks - 2:
                while side_work:
                    next_side()
                for lane in (act, dve, pool, sp):
                    lane.hold(side_done)
                k_stack.append(early("k_stack0", [ROWS, GH, L], fp32r))
                q_stack += [early(f"q_stack{i}", [ROWS, GH, CH], fp32r) for i in range(2)]
                v_group.append(early("v_group0", [P, KT, P]))
                max_part = early("max_part", [P, N_MAX])
                max_q = early("max_q", [P, GH * TT])
                negmax_hi = early("negmax_hi", [GH * TT, P], fp32r)
                negmax_lo = early("negmax_lo", [GH * TT, P], fp32r)
                prob_sum = early("prob_sum", [P, GH, CH])
                wproj_hi = wproj_region("wproj_hi", [P, KD, D], fp32r)
                wproj_lo = wproj_region("wproj_lo", [P, KD, D], fp32r)
                set_ones_rows(0)
                t_raw = []
                early_loads = [
                    lambda: load_keys(0), lambda: load_q(0), lambda: load_q(1),
                    lambda: load_values(0),
                    lambda: t_raw.append(sp.move(
                        prob_sum[:, :, :], t["Wproj"].rearrange("(k p) n -> p k n", p=P),
                        a_wp2))]
            if last_chunk:
                smax_banks.free[0], smax_banks.free[1] = tr_banks.free
                smax_banks.free[2] = bank_free[SIDE_BANK]
                t_wproj += split_weights(prob_sum[:, :, :], wproj_hi[:, :, :],
                                         wproj_lo[:, :, :], t_raw)
                prob_sum_read[:] = t_wproj
            for j in range(2 * KD):
                i_mm, bank, free = mm_banks.take()
                t_mm = three_pass(psum[:, bank, :], [
                    (wqkv_hi[:, k, j * P:(j + 1) * P], wqkv_lo[:, k, j * P:(j + 1) * P],
                     hi[:, k, :], lo[:, k, :]) for k in range(KD)],
                    after=free + t_h[c] + t_wqkv[(j + 1) * P > RAW],
                    between=early_maximum if last_chunk else None)
                i_o, o, o_free = qk_out.take()
                bias = cols[:, BQK + j:BQK + j + 1]
                t_a = act.put(lambda e, o=o, bank=bank, bias=bias: e.activation(
                    o[:, 0, :], psum[:, bank, :], ACT.Identity, bias=bias),
                    after=[t_mm, t_cols] + o_free)
                t_b = dve.put(lambda e, o=o, bank=bank, bias=bias: e.scalar_tensor_tensor(
                    o[:, 1, :], psum[:, bank, :], bias, o[:, 0, :].bitcast(fp32),
                    ALU.add, ALU.subtract), after=[t_a] + o_free)
                mm_banks.free[i_mm] = [t_b]
                t_st = sp.move(qk_dram[b, :, j * P:(j + 1) * P, half * CH:(half + 1) * CH]
                               .rearrange("s p t -> p s t"), o[:, :, :], a_qk[i_o],
                               after=[t_a, t_b])
                qk_out.free[i_o] = [t_st]
                if j == 1:
                    norm1(c + 1)
                if j >= KD and c + 1 < n_chunks:
                    feature_block(c + 1, j - KD)()
                if early_loads:
                    early_loads.pop(0)()
                if j not in (1, 2):
                    next_side()
            if last_chunk:
                send_max()
            for i in range(TT):
                i_mm, bank, free = mm_banks.take()
                t_mm = three_pass(psum[:, bank, :], [
                    (hi[:, k, i * P:(i + 1) * P], lo[:, k, i * P:(i + 1) * P],
                     wqkv_hi[:, k, 2 * D:3 * D], wqkv_lo[:, k, 2 * D:3 * D]) for k in range(KD)],
                    after=free,
                    between=early_maximum if last_chunk else None)
                i_o, o, o_free = v_out.take()
                t_v = dve.put(lambda e, o=o, bank=bank: e.tensor_tensor(
                    o[:, :], psum[:, bank, :], bv[:, :], ALU.add), after=[t_mm, t_bv] + o_free)
                mm_banks.free[i_mm] = [t_v]
                at = half * CH + i * P
                t_st = sp.move(v_dram[b, at:at + P, :], o[:, :], a_v[i_o], after=[t_v])
                v_out.free[i_o] = [t_st]
            hT.free[i_h] = [t_mm]
        s1_done = everything()
        s1.close()

        for lane in (pool, sp):
            lane.hold(s1_done)
        for lane in (act, dve):
            lane.hold([(x.done, x.count) for x in (pe, act, dve)])
        for i in range(len(ST)):
            st_banks.free[i] = mm_banks.free[i]
        s2 = sb = Region()
        k_stack.append(sb("k_stack1", [ROWS, GH, L], fp32r))
        set_ones_rows(1)
        q_stack.append(sb("q_stack2", [ROWS, GH, CH], fp32r))
        v_group.append(sb("v_group1", [P, KT, P]))
        probs = [sb(f"probs{i}", [P, GH, 2, CH]) for i in range(3)]
        project_region = Region(top=True)
        sb = project_region
        attn = [None, None]
        attn[(B - 1) % 2] = sb("attn_last", [P, NG, L])
        attn[B % 2] = s2("attn_other", [P, NG, L])
        attn_hi = [sb(f"attn_hi{i}", [P, NG, P], fp32r) for i in range(2)]
        attn_lo = [sb(f"attn_lo{i}", [P, NG, P], fp32r) for i in range(2)]
        x_res = [sb(f"x_res{i}", [P, D]) for i in range(XR)]
        x1_out = [sb(f"x1_out{i}", [P, D]) for i in range(2)]
        gates = [None, None]
        gates[(B - 1) % 2] = sb("gates_last", [P, 2, D])
        gates[B % 2] = s2("gates_other", [P, 2, D])
        den_inv = sb("den_inv", [P, CH])
        weighted = [sb(f"weighted{i}", [P, CH]) for i in range(2)]

        probs_read = [[], [], []]
        attn_hi_read = [[], []]
        attn_read = [[], []]
        attn_done = {}
        pv_free, den_free = list(mm_banks.free[3]), list(mm_banks.free[4])
        x1_read = [[], []]
        xr_read = [[] for _ in range(XR)]
        t_xr = {}

        def load_x_res(n):
            b, i = divmod(n, KT)
            t_xr[n] = sp.move(x_res[n % XR][:, :], t["x"][b, i * P:(i + 1) * P, :], a_xr[n % XR],
                              after=xr_read[n % XR])

        t_xg = {}

        def add_gated_bias(n):
            b = n // KT
            t_xg[n] = pool.put(lambda e: e.tensor_tensor(
                x_res[n % XR][:, :], x_res[n % XR][:, :], gates[b % 2][:, 1, :], ALU.add),
                after=[t_xr[n], t_g[b]])

        def project(n, ready=None, ring=None):
            b, i = divmod(n, KT)
            src = attn[b % 2]
            cut = slice(i * P, (i + 1) * P)
            hi, lo = attn_hi[n % 2], attn_lo[n % 2]
            read = attn_hi_read[n % 2]
            t_hi = act.put(lambda e: e.activation(hi[:, :, :], src[:, :, cut], ACT.Copy),
                           after=(ready or attn_done[b]) + read)
            t_lo = dve.put(lambda e: e.tensor_tensor(
                lo[:, :, :], src[:, :, cut], hi[:, :, :].bitcast(fp32), ALU.subtract),
                after=[t_hi] + read)
            if i == KT - 1:
                attn_read[b % 2] = [t_hi, t_lo]
            used = []

            def multiply():
                i_b, bank, free = ring.take() if ring else (None, DEN_BANK, den_free)
                t_mm = products(bank, free + [t_hi, t_lo] + t_wproj)
                attn_hi_read[n % 2] = [t_mm]
                used.extend((i_b, bank, t_mm))

            def products(bank, after):
                for k in range(KD):
                    for a, w in ((hi, wproj_hi), (hi, wproj_lo), (lo, wproj_hi)):
                        last = k == KD - 1 and a is lo
                        t_mm = pe.put(lambda e, k=k, a=a, w=w, last=last: e.matmul(
                            psum[:, bank, :], a[:, k, :], w[:, k, :],
                            start=(k == 0 and a is hi and w is wproj_hi), stop=last),
                            after=after, signal=last)
                return t_mm

            def residual():
                i_b, bank, t_mm = used
                o = x1_out[n % 2]
                t_y = dve.put(lambda e: e.tensor_tensor(
                    o[:, :], psum[:, bank, :], gates[b % 2][:, 0, :], ALU.mult),
                    after=[t_mm, t_g[b]] + x1_read[n % 2])
                if ring:
                    ring.free[i_b] = [t_y]
                else:
                    den_free[:] = [t_y]
                t_x1 = dve.put(lambda e: e.tensor_tensor(
                    o[:, :], o[:, :], x_res[n % XR][:, :], ALU.add), after=[t_y, t_xg[n]])
                xr_read[n % XR] = [t_x1]
                if i == KT - 1:
                    gates_read[b % 2] = [t_x1]
                x1_read[n % 2] = [sp.move(x1_dram[b, i * P:(i + 1) * P, :], o[:, :], a_x1[n % 2],
                                          after=[t_x1])]

            return multiply, residual

        def slot(u, s):
            return (u * (KT // 2) + s) % len(probs)

        def value_products(u, s, j):
            b, g, _ = units[u]
            G = b * NG + g
            kt = 2 * s + j
            pb = probs[slot(u, s)]
            for h in range(GH):
                t_pv = pe.put(lambda e, h=h: e.matmul(
                    psum[h * HD:(h + 1) * HD, PV_BANK, :],
                    v_group[G % 2][:, kt, h * HD:(h + 1) * HD], pb[:, h, j, :],
                    start=(kt == 0), stop=(kt == KT - 1)),
                    after=(t_p[u, s] + [t_vg[G]] + pv_free) if h == 0 else (),
                    signal=(h == GH - 1))
            return t_pv

        load_gates(0)
        SUMMED = STEPS - 1
        LAST = KT // 2 - 1
        PROJ_LAG = PER_B + 1
        t_weighted, t_den = {}, {}
        weighted_read = [[], []]

        def sum_probs(u, s, t_p):
            pb = probs[slot(u, s)]
            if s == 0:
                t_sum = pool.put(lambda e: e.tensor_tensor(
                    prob_sum[:, :, :], pb[:, :, 0, :], pb[:, :, 1, :], ALU.add),
                    after=t_p + prob_sum_read)
            else:
                for j in range(2):
                    t_sum = pool.put(lambda e, j=j: e.tensor_tensor(
                        prob_sum[:, :, :], prob_sum[:, :, :], pb[:, :, j, :], ALU.add),
                        after=t_p + t_summed)
                    t_summed[:] = [t_sum]
            t_summed[:] = [t_sum]

        t_summed = []

        def denominators(u, n, last):
            term = prob_sum[:, :, :] if last else probs[slot(u, LAST)][:, :, n, :]
            for h in range(GH):
                t = pe.put(lambda e, h=h: e.matmul(
                    psum[h * HD:(h + 1) * HD, DEN_BANK, :], ones[:, :], term[:, h, :],
                    start=(n == 0), stop=last),
                    after=(t_summed if last else ()) or [t_ones] + den_free,
                    signal=(h == GH - 1))
            t_den[u] = t
            if last:
                prob_sum_read[:] = [t]
            else:
                probs_read[slot(u, LAST)] = probs_read[slot(u, LAST)] + [t]

        def normalise_attention(u):
            b, g, half = units[u]
            pieces = 4
            for n in range(pieces):
                cut = slice(n * CH // pieces, (n + 1) * CH // pieces)
                t_i = dve.put(lambda e, cut=cut: e.reciprocal(
                    den_inv[:, cut], psum[:, DEN_BANK, cut]), after=[t_den[u]] + den_inv_read)
                if n == pieces - 1:
                    den_free[:] = [t_i]
                yield
            t_n = dve.put(lambda e: e.tensor_tensor(
                attn[b % 2][:, g, half * CH:(half + 1) * CH], weighted[u % 2][:, :],
                den_inv[:, :], ALU.mult), after=[t_i, t_weighted[u]] + attn_read[b % 2])
            den_inv_read[:] = [t_n]
            weighted_read[u % 2] = [t_n]
            attn_done[b] = [t_n]
            yield

        den_inv_read = []

        def last_values(u):
            for j in range(2):
                t_pv = value_products(u, LAST, j)
            probs_read[slot(u, LAST)] = [t_pv]
            b, g, half = units[u]
            if half == NCH - 1:
                vg_free[(b * NG + g) % 2] = [t_pv]
            t_weighted[u] = act.put(lambda e: e.activation(
                weighted[u % 2][:, :], psum[:, PV_BANK, :], ACT.Copy),
                after=[t_pv] + weighted_read[u % 2])
            pv_free[:] = [t_weighted[u]]

        residuals = []
        t_p = {}
        for u, (b, g, half) in enumerate(units):
            G = b * NG + g
            if half == 0 and (G + 1) * NCH < NU:
                load_keys(G + 1)
            if u + 2 < NU:
                load_q(u + 2)
            if u % PER_B == 2 and b >= 1:
                load_gates(b)
            tile = u - PROJ_LAG
            if tile >= 0:
                load_x_res(tile)
            normalisation, projection = [], []
            for s in range(STEPS):
                pb = probs[slot(u, s)]
                t_p[u, s] = []

                def scores(h, j, s=s, pb=pb):
                    q, k = q_stack[u % 3], k_stack[G % 2]
                    kt = 2 * s + j
                    i_b, bank, free = st_banks.take()
                    t_mm = pe.put(lambda e: e.matmul(
                        psum[:, bank, :], k[0:ROWS, h, kt * P:(kt + 1) * P],
                        q[0:ROWS, h, :], start=True, stop=True),
                        after=free + [t_m[u], t_q[u], t_k[G], t_ones_rows[G % 2]])
                    t_e = act.put(lambda e: e.activation(
                        pb[:, h, j, :], psum[:, bank, :], ACT.Exp, scale=SCALE),
                        after=[t_mm] + probs_read[slot(u, s)])
                    st_banks.free[i_b] = [t_e]
                    t_p[u, s].append(t_e)
                    if s == LAST and h == GH - 1 and j == 1:
                        q_free[u % 3] = [t_mm]
                        if half == NCH - 1:
                            k_free[G % 2] = [t_mm]

                def values(j, s=s):
                    t_pv = value_products(u, s - 1, j)
                    if j == 1:
                        probs_read[slot(u, s - 1)] = [t_pv] + t_summed

                def step_work(half_step):
                    at = (s, half_step)
                    if at == (2, 0) and u == 0:
                        act.hold(s1_done)
                        dve.hold(s1_done)
                    if at == (0, 0):
                        if u > 0:
                            last_values(u - 1)
                            if residuals:
                                residuals.pop()()
                        if half == 0 and (G + 1) * NCH < NU:
                            load_values(G + 1)
                    if at == (0, 1) and u > 0:
                        denominators(u - 1, 0, False)
                        denominators(u - 1, 1, False)
                    if at == (1, 0):
                        if u > 0:
                            denominators(u - 1, 2, True)
                            normalisation.append(normalise_attention(u - 1))
                            next(normalisation[0])
                        if tile >= 0:
                            add_gated_bias(tile)
                            projection.extend(project(tile))
                        sum_probs(u, 0, t_p[u, 0])
                    if s in (1, 2):
                        values(half_step)
                    if at == (3, 0):
                        values(0)
                        values(1)
                    if at in ((1, 1), (2, 0), (2, 1), (3, 0)) and normalisation:
                        next(normalisation[0])
                    if at == (3, 1) and tile >= 0:
                        multiply, residual = projection
                        multiply()
                        residuals.append(residual)

                for half_step in range(2):
                    tiles = iter(range(4))
                    for what in ORDER[s][half_step]:
                        if what == "s":
                            n = next(tiles)
                            scores(2 * half_step + n // 2, n % 2)
                        elif what == "m":
                            next_maximum()
                        elif what == "*":
                            step_work(half_step)
                        elif to_send:
                            send_max()
                if 0 < s < SUMMED:
                    sum_probs(u, s, t_p[u, s])
        tail = list(range(NU - PROJ_LAG, B * KT))
        assert tail[0] >= TT, "stage 3 starts with a chunk that the tail would write"
        before_last = attn_done[B - 1]

        for tile in tail[:XR - 1]:
            load_x_res(tile)
        add_gated_bias(tail[0])
        first = project(tail[0], ring=smax_banks)
        last_values(NU - 1)
        residuals.pop()()
        load_x_res(tail[XR - 1])
        denominators(NU - 1, 0, False)
        denominators(NU - 1, 1, False)
        for part in first:
            part()
        load_x_res(tail[XR])
        denominators(NU - 1, 2, True)
        s2_done = everything()
        add_gated_bias(tail[1])
        following = project(tail[1], before_last, smax_banks)
        for _ in normalise_attention(NU - 1):
            pass
        for region in (s2, early):
            region.close()
        for lane in (act, dve, pool, sp):
            lane.hold(s2_done)

        s3 = sb = Region()
        HB = 2
        NPC = KM // HB
        w1_hi, w1_lo, w2_hi, w2_lo = [], [], [], []
        w_raw_region = Region(top=True)
        w_raw = Ring([w_raw_region(f"w_raw{i}", [P, HB * D]) for i in range(3)])
        a_wr = [arrival(f"a_wr{i}") for i in range(3)]
        t_w1, t_w2 = [], []

        def piece_buffers(count):
            for _ in range(count):
                n = len(w1_hi)
                for part, name in ((w1_hi, "w1_hi"), (w1_lo, "w1_lo")):
                    part.append(s3(f"{name}{n}", [P, KD, HB * P], fp32r))
                for part, name in ((w2_hi, "w2_hi"), (w2_lo, "w2_lo")):
                    part.append(s3(f"{name}{n}", [P, HB, D], fp32r))

        def load_weights(m):
            n, which = divmod(m, 2)
            i_r, raw, free = w_raw.take()
            at = n * HB
            if which == 0:
                view = raw[:, :].rearrange("p (a b) -> p a b", a=KD)
                src = t["W1"].rearrange("(k p) m -> p k m", p=P)[:, :, at * P:(at + HB) * P]
                hi, lo, done = w1_hi, w1_lo, t_w1
            else:
                view = raw[:, :].rearrange("p (a b) -> p a b", a=HB)
                src = t["W2"].rearrange("(k p) m -> p k m", p=P)[:, at:at + HB, :]
                hi, lo, done = w2_hi, w2_lo, t_w2
            t_r = sp.move(view, src, a_wr[i_r], after=free)

            def split():
                t_s = split_weights(view, hi[n][:, :, :], lo[n][:, :, :], [t_r], pool)
                w_raw.free[i_r] = t_s
                done.append(t_s)

            return split

        pieces = iter(range(2 * NPC))
        loaded = []

        def next_weights():
            while len(loaded) < len(w_raw.buffers):
                m = next(pieces, None)
                if m is None:
                    break
                loaded.append(load_weights(m))
            loaded.pop(0)()

        piece_buffers(NPC // 2)
        loaded.append(load_weights(next(pieces)))
        x1 = [sb("x1_0", [P, TT, D])]
        xn_mlp = sb("xn2", [P, TT, D])
        h_hi = sb("h2_hi", [P, KD, CH], fp32r)
        h_lo = sb("h2_lo", [P, KD, CH], fp32r)
        work = Ring([sb(f"work{i}", [P, CH]) for i in range(4)])
        g_parts = Ring([sb(f"g_parts{i}", [P, 2, CH], fp32r) for i in range(3)])
        rows3 = sb("rows3", [P, 4, D])
        stats = sb("stats2", [P, TT, 6])
        moments = sb("moments2", [P, TT, 2])
        inv_std = sb("inv_std2", [P, TT])
        square_sum = sb("square_sum", [P, TT])
        a_x1r = [arrival(f"a_x1r{i}") for i in range(2)]
        a_r3 = arrival("a_rows3")
        a_y = [arrival(f"a_y{i}") for i in range(2)]
        ACC = (0, 1, 2, 3)
        tr_banks = Ring([4, 5])
        up_banks = Ring([6, 7])
        x1_free = [[], []]
        acc_free = [[] for _ in ACC]
        h_free, rows3_free, xn_read = [], [], []
        square_read = []
        t_x1, t_rows3, t_h = {}, {}, {}

        x1_written = []

        def load_x1(c):
            b, half = divmod(c, NCH)
            t_x1[c] = sp.move(x1[c % 2][:, :, :],
                              x1_dram[b, half * CH:(half + 1) * CH, :]
                              .rearrange("(t p) d -> p t d", p=P), a_x1r[c % 2],
                              after=x1_free[c % 2] + x1_written)

        def load_rows3(b):
            for n in range(4):
                t_rows3[b] = sp.move(rows3[:, n, :],
                                     rows_dram[GATE2 + n, b].partition_broadcast(P), a_r3,
                                     after=rows3_free)

        def add_bias(c):
            b = c // NCH
            return pool.put(lambda e: e.tensor_tensor(
                x1[c % 2][:, :, :], x1[c % 2][:, :, :],
                rows3[:, 1, :].unsqueeze(1).to_broadcast([P, TT, D]), ALU.add),
                after=[t_rows3[b]] + t_norm[c])

        t_norm, t_biased = {}, {}
        lag = []

        def up(c, i):
            piece, at = divmod(i, HB)
            cols_of_i = slice(at * P, (at + 1) * P)
            i_b, bank, free = up_banks.take()
            t_mm = three_pass(psum[:, bank, :], [
                (w1_hi[piece][:, k, cols_of_i], w1_lo[piece][:, k, cols_of_i],
                 h_hi[:, k, :], h_lo[:, k, :]) for k in range(KD)],
                after=free + t_h[c] + t_w1[piece])
            if i == KM - 1:
                h_free[:] = [t_mm]
            i_w, w, w_free = work.take()
            i_g, gp, g_free = g_parts.take()
            bias = cols[:, B1 + i:B1 + i + 1]
            t_f = act.put(lambda e: e.activation(w[:, :], psum[:, bank, :], ACT.Gelu, bias=bias),
                          after=[t_mm] + w_free)
            t_hi = act.put(lambda e: e.activation(gp[:, 0, :], psum[:, bank, :], ACT.Gelu,
                                                  bias=bias), after=g_free)
            up_banks.free[i_b] = [t_hi]
            t_lo = dve.put(lambda e: e.tensor_tensor(
                gp[:, 1, :], w[:, :], gp[:, 0, :].bitcast(fp32), ALU.subtract),
                after=[t_f, t_hi] + g_free)
            work.free[i_w] = [t_lo]

            def down():
                for n in range(TT):
                    cut = slice(n * P, (n + 1) * P)
                    pairs = ((0, w2_hi[piece]), (0, w2_lo[piece]), (1, w2_hi[piece]))
                    for m, (part, w2) in enumerate(pairs):
                        last = i == KM - 1 and m == 2
                        t_d = pe.put(lambda e, n=n, cut=cut, part=part, w2=w2, m=m, last=last:
                                     e.matmul(psum[:, ACC[n], :], gp[:, part, cut],
                                              w2[:, at, :], start=(i == 0 and m == 0),
                                              stop=last),
                                     after=([t_hi, t_lo] + t_w2[piece]
                                            + (acc_free[n] if i == 0 else [])) if m == 0 else (),
                                     signal=m == 2)
                    t_down[n] = t_d
                g_parts.free[i_g] = [t_d]

            return down

        t_down = [None] * TT

        def finish_first(c):
            b = c // NCH
            t_x2 = []
            for n in range(TT):
                i_w, w, w_free = work.take()
                t_y = dve.put(lambda e, n=n, w=w: e.tensor_tensor(
                    w[:, :], psum[:, ACC[n], :], rows3[:, 0, :], ALU.mult),
                    after=[t_down[n], t_rows3[b]] + w_free)
                acc_free[n] = [t_y]
                t_x2.append(dve.put(lambda e, n=n, w=w: e.tensor_tensor(
                    x1[c % 2][:, n, :], x1[c % 2][:, n, :], w[:, :], ALU.add),
                    after=[t_y, t_biased[c]]))
                work.free[i_w] = [t_x2[-1]]
            return t_x2

        def finish_second(c, t_x2):
            for n in range(TT):
                i_w, w, w_free = work.take()
                t_s = act.put(lambda e, n=n, w=w: e.activation(
                    w[:, :], x1[c % 2][:, n, :], ACT.Square,
                    accum_out=square_sum[:, n:n + 1]), after=[t_x2[n]] + w_free + square_read)
                work.free[i_w] = [t_s]
            t_r = dve.put(lambda e: e.tensor_scalar(
                square_sum[:, :], square_sum[:, :], 1.0 / D, RMS_EPS, ALU.mult, ALU.add),
                after=[t_s])
            t_r = dve.put(lambda e: e.reciprocal(square_sum[:, :], square_sum[:, :]),
                          after=[t_r])
            return act.put(lambda e: e.activation(square_sum[:, :], square_sum[:, :], ACT.Sqrt),
                           after=[t_r])

        def finish_third(c, t_r, n):
            b, half = divmod(c, NCH)
            i_y, y, y_free = y_out.take()
            t_a = dve.put(lambda e: e.scalar_tensor_tensor(
                y[:, :], x1[c % 2][:, n, :], square_sum[:, n:n + 1], rows3[:, 2, :],
                ALU.mult, ALU.mult), after=[t_r, t_rows3[b]] + y_free)
            t_b = pool.put(lambda e: e.tensor_tensor(y[:, :], y[:, :], rows3[:, 3, :], ALU.add),
                           after=[t_a])
            at = half * CH + n * P
            t_st = sp.move(out[b, at:at + P, :], y[:, :], a_y[i_y], after=[t_b])
            y_out.free[i_y] = [t_st]
            if n == TT - 1:
                square_read[:] = [t_a]
                x1_free[c % 2] = [t_a]
                rows3_free[:] = [t_b]

        def norm2(c):
            t_norm[c] = normalise(x1[c % 2], xn_mlp, stats, moments, inv_std, [t_x1[c]], xn_read)

        def transpose_h(c, blocks):
            b = c // NCH
            if blocks[0] == 0:
                t_h[c] = []
                xn_read[:] = []
            subtractions = []
            for f in blocks:
                i_tr, bank, free = tr_banks.take()
                for i in range(TT):
                    t_tr = pe.put(lambda e, i=i, f=f, bank=bank: e.transpose(
                        psum[:, bank, i * P:(i + 1) * P], xn_mlp[:, i, f * P:(f + 1) * P],
                        ident[:, :]), after=t_norm[c] + free, signal=(i == TT - 1))
                xn_read.append(t_tr)
                i_w, w, w_free = work.take()
                t_f = dve.put(lambda e, f=f, bank=bank, w=w: e.tensor_scalar(
                    w[:, :], psum[:, bank, :], ln_scale[:, 1, f, b:b + 1],
                    ln_shift[:, 1, f, b:b + 1], ALU.mult, ALU.add),
                    after=[t_tr] + t_ln2 + w_free)
                tr_banks.free[i_tr] = [t_f]
                t_hi = act.put(lambda e, f=f, w=w: e.activation(
                    h_hi[:, f, :], w[:, :], ACT.Copy), after=[t_f] + h_free)
                subtractions.append((f, i_w, w, t_hi))
            for f, i_w, w, t_hi in subtractions:
                t_lo = dve.put(lambda e, f=f, w=w: e.tensor_tensor(
                    h_lo[:, f, :], w[:, :], h_hi[:, f, :].bitcast(fp32), ALU.subtract),
                    after=[t_hi] + h_free)
                work.free[i_w] = [t_lo]
                t_h[c] += [t_hi, t_lo]

        load_x1(0)
        loaded.append(load_weights(next(pieces)))
        tr_banks.free[:] = st_banks.free[1:3]
        up_banks.free[:] = [list(pv_free), list(den_free)]
        for n, tile in enumerate(tail[1:], 1):
            now = following
            if n + 1 < len(tail):
                after_it = tail[n + 1]
                add_gated_bias(after_it)
                following = project(
                    after_it, before_last if after_it % KT < KT // 2 else None, smax_banks)
            for part in now:
                part()
            if n + XR < len(tail):
                load_x_res(tail[n + XR])
            if n == 3:
                norm2(0)
            if n in (5, 6):
                transpose_h(0, (2 * n - 10, 2 * n - 9))
            if len(t_w2) < NPC // 2:
                next_weights()
        for m in range(TT - 1):
            acc_free[m] = smax_banks.free[m]
        acc_free[TT - 1] = st_banks.free[0]
        tail_done = everything()
        load_rows3(0)
        x1_written += tail_done
        for region in (wproj_region, project_region):
            region.close()
        while len(t_w2) < NPC // 2:
            next_weights()
        piece_buffers(NPC - NPC // 2)
        for c in range(n_chunks + 1):
            b, half = divmod(c, NCH)
            live = c < n_chunks
            for n in range(2):
                if live and c > 0:
                    transpose_h(c, (2 * n, 2 * n + 1))
                if lag:
                    lag.pop(0)()
            if c >= 1:
                t_x2 = finish_first(c - 1)
            if live:
                for i in range(KM):
                    if c == 0 and i >= 2 and len(t_w2) < NPC:
                        if i == 2:
                            for lane in (act, dve, pool):
                                lane.hold(tail_done)
                        next_weights()
                        if len(t_w2) == NPC:
                            raw_free = [x for free in w_raw.free for x in free]
                            w_raw_region.close()
                            x1.append(s3("x1_1", [P, TT, D]))
                            y_out = Ring([s3(f"y_out{i}", [P, D]) for i in range(2)])
                            x1_free[1] = raw_free
                            y_out.free[:] = [raw_free, raw_free]
                    lag.append(up(c, i))
                    if len(lag) > 2:
                        lag.pop(0)()
                    if c >= 1 and i == 2:
                        t_r = finish_second(c - 1, t_x2)
                    if c >= 1 and 3 <= i < 3 + TT:
                        finish_third(c - 1, t_r, i - 3)
                    if i == 10 and c + 1 < n_chunks:
                        load_x1(c + 1)
                    if i == 9 and c > 0 and half == 0:
                        load_rows3(b)
                    if i == 10:
                        t_biased[c] = add_bias(c)
                    if i == 12 and c + 1 < n_chunks:
                        norm2(c + 1)
            else:
                t_r = finish_second(c - 1, t_x2)
                for n in range(TT):
                    finish_third(c - 1, t_r, n)
        s3.close()

        block = whole.enter_context(nc.Block())
        final = [(a.sem, a.value) for a in arrivals if a.value]
        for s_, v_ in final:
            sp.todo.append(lambda e, s_=s_, v_=v_: e.wait_ge(s_, v_))

        @block.sync
        def _(engine):
            sp.run(engine)

        @block.scalar
        def _(engine):
            act.run(engine)

        @block.vector
        def _(engine):
            dve.run(engine)

        @block.gpsimd
        def _(engine):
            pool.run(engine)

        @block.tensor
        def _(engine):
            pe.run(engine)


_SHORT = {"cond_1024": "cond"}


def kernel(**inputs):
    import concourse.bacc as bacc
    from concourse.bass_utils import run_bass_kernel_spmd

    nc = bacc.Bacc("TRN2", target_bir_lowering=False, num_devices=1)
    arrays, tensors = {}, {}
    for name, a in inputs.items():
        short = _SHORT.get(name, name.replace("L0_cond_", "").replace("L1_cond_", ""))
        a = np.ascontiguousarray(a)
        arrays[f"in_{short}"] = a
        tensors[short] = nc.dram_tensor(f"in_{short}", a.shape, mybir.dt.from_np(a.dtype),
                                        kind="ExternalInput").ap()
    x = arrays["in_x"]
    out = nc.dram_tensor("out_0", x.shape, mybir.dt.from_np(x.dtype), kind="ExternalOutput").ap()
    build_block(nc, tensors, out)
    result = run_bass_kernel_spmd(nc, [arrays], core_ids=[0])
    return result.results[0]["out_0"]
```
